# Optimizing a Trainium2 kernel written in Bass

```python
import numpy as np
import jax
import jax.numpy as jnp

def _softmax(x, axis=-1):
    return jax.nn.softmax(x, axis=axis)

def _gelu(x):
    return jax.nn.gelu(x, approximate=True)

def _silu(x):
    return jax.nn.silu(x)

def _sigmoid(x):
    return jax.nn.sigmoid(x)

def _layernorm(x, axis=-1, eps=1e-05):
    m = jnp.mean(x, axis=axis, keepdims=True)
    v = jnp.var(x, axis=axis, keepdims=True)
    return (x - m) / jnp.sqrt(v + eps)

def _scatter_add(tgt, idx, src, axis=0):
    return tgt.at[idx].add(src)

def _segment_sum(src, seg, n):
    return jax.ops.segment_sum(src, seg, n)
kernel_name = 'mk_prb_d1_jaxref_r4_11364c'

def setup_inputs(seed: int=0):
    np.random.seed(seed)
    _w = jnp.asarray

    def _L0_attn_setup():
        import jax, jax.numpy as jnp
        import numpy as np
        DIM = 256
        HEADS = 16
        HEAD_DIM = DIM // HEADS
        B, S = (4, 1024)
        key = jax.random.key(seed)
        ks = jax.random.split(key, 8)
        sc = 1.0 / np.sqrt(DIM)
        return {'x': jax.random.normal(ks[0], (B, S, DIM), dtype=jnp.float32), 'Wq': jax.random.normal(ks[1], (DIM, DIM), dtype=jnp.float32) * sc, 'Wk': jax.random.normal(ks[2], (DIM, DIM), dtype=jnp.float32) * sc, 'Wv': jax.random.normal(ks[3], (DIM, DIM), dtype=jnp.float32) * sc, 'Wp': jax.random.normal(ks[4], (DIM, DIM), dtype=jnp.float32) * sc, 'bp': jnp.zeros((DIM,), dtype=jnp.float32), 'conv_w': jax.random.normal(ks[5], (DIM, 3), dtype=jnp.float32) * (1.0 / np.sqrt(3.0)), 'conv_b': jnp.zeros((DIM,), dtype=jnp.float32)}
    _L0_attn_in = _L0_attn_setup()

    def _L0_ffn_setup():
        import jax, jax.numpy as jnp
        import numpy as np
        DIM = 256
        HIDDEN = 768
        SCALE = 1.0 / 127.0

        def _dequant(w_int, dtype):
            return w_int.astype(dtype) * jnp.asarray(SCALE, dtype)
        key = jax.random.key(seed)
        k_x, k_g, k_u, k_d = jax.random.split(key, 4)
        x = jax.random.normal(k_x, (4, 512, DIM), dtype=jnp.float32)
        w_gate = jax.random.randint(k_g, (HIDDEN, DIM), -127, 128, dtype=jnp.int32)
        w_up = jax.random.randint(k_u, (HIDDEN, DIM), -127, 128, dtype=jnp.int32)
        w_down = jax.random.randint(k_d, (DIM, HIDDEN), -127, 128, dtype=jnp.int32)
        return {'x': x, 'w_gate': w_gate, 'w_up': w_up, 'w_down': w_down}
    _L0_ffn_in = _L0_ffn_setup()
    _d = {'L0_attn_x': _L0_attn_in['x'], 'L0_attn_Wq': _L0_attn_in['Wq'], 'L0_attn_Wk': _L0_attn_in['Wk'], 'L0_attn_Wv': _L0_attn_in['Wv'], 'L0_attn_Wp': _L0_attn_in['Wp'], 'L0_attn_bp': _L0_attn_in['bp'], 'L0_attn_conv_w': _L0_attn_in['conv_w'], 'L0_attn_conv_b': _L0_attn_in['conv_b'], 'L0_ffn_w_gate': _L0_ffn_in['w_gate'], 'L0_ffn_w_up': _L0_ffn_in['w_up'], 'L0_ffn_w_down': _L0_ffn_in['w_down']}
    _x0 = _d['L0_attn_x']
    _d['L0_attn_x'] = jax.random.normal(jax.random.fold_in(jax.random.key(seed), 1), (8, 1024, 256), dtype=_x0.dtype)
    del _x0
    return _d

def reference(L0_attn_x, L0_attn_Wq, L0_attn_Wk, L0_attn_Wv, L0_attn_Wp, L0_attn_bp, L0_attn_conv_w, L0_attn_conv_b, L0_ffn_w_gate, L0_ffn_w_up, L0_ffn_w_down):

    def _L0_attn_ref(x, Wq, Wk, Wv, Wp, bp, conv_w, conv_b):
        import jax, jax.numpy as jnp
        import numpy as np
        DIM = 256
        HEADS = 16
        HEAD_DIM = DIM // HEADS
        B, S = (4, 1024)
        b, s, d = x.shape

        def split_heads(t):
            return t.reshape(b, s, HEADS, HEAD_DIM).transpose(0, 2, 1, 3)
        q = split_heads(x @ Wq.T)
        k = split_heads(x @ Wk.T)
        v = split_heads(x @ Wv.T)
        q = jax.nn.elu(q) + 1.0
        k = jax.nn.elu(k) + 1.0
        kv_state = jnp.einsum('bhnd,bhne->bhde', k, v)
        k_state = k.sum(axis=2)
        attn_out = jnp.einsum('bhnd,bhde->bhne', q, kv_state)
        denom = jnp.maximum(jnp.einsum('bhnd,bhd->bhn', q, k_state), 1e-06)[..., None]
        attn_out = (attn_out / denom).transpose(0, 2, 1, 3).reshape(b, s, d)
        xp = jnp.pad(x, ((0, 0), (1, 1), (0, 0)))
        local = xp[:, :-2, :] * conv_w[:, 0] + xp[:, 1:-1, :] * conv_w[:, 1] + xp[:, 2:, :] * conv_w[:, 2] + conv_b
        return (attn_out + local) @ Wp.T + bp

    def _L0_ffn_ref(x, w_gate, w_up, w_down):
        import jax, jax.numpy as jnp
        import numpy as np
        DIM = 256
        HIDDEN = 768
        SCALE = 1.0 / 127.0

        def _dequant(w_int, dtype):
            return w_int.astype(dtype) * jnp.asarray(SCALE, dtype)
        wg = _dequant(w_gate, x.dtype)
        wu = _dequant(w_up, x.dtype)
        wd = _dequant(w_down, x.dtype)
        gate = jnp.einsum('bsd,hd->bsh', x, wg)
        up = jnp.einsum('bsd,hd->bsh', x, wu)
        h = jax.nn.silu(gate) * up
        return jnp.einsum('bsh,dh->bsd', h, wd)
    x = L0_attn_x
    xn = _layernorm(x, axis=-1)
    x = x + _L0_attn_ref(xn, L0_attn_Wq, L0_attn_Wk, L0_attn_Wv, L0_attn_Wp, L0_attn_bp, L0_attn_conv_w, L0_attn_conv_b) + _L0_ffn_ref(xn, L0_ffn_w_gate, L0_ffn_w_up, L0_ffn_w_down)
    return x

_drawn_inputs = setup_inputs


def setup_inputs(seed=0):
    import zlib

    import numpy as np

    out = dict(_drawn_inputs(seed))
    spreads = {'L0_attn_bp': (0.0, 2.0), 'L0_attn_conv_b': (0.0, 2.0)}
    factors = {'L0_attn_Wq': 64.0,
     'L0_attn_Wk': 64.0,
     'L0_attn_Wv': 64.0,
     'L0_attn_Wp': 8.0,
     'L0_attn_conv_w': 8.0}
    for name, (base, spread) in spreads.items():
        noise = np.random.default_rng([zlib.crc32(name.encode()), seed]).standard_normal(out[name].shape)
        drawn = base * np.exp(spread * noise) if base else spread * noise
        out[name] = jnp.asarray(drawn.astype(out[name].dtype))
    for name, factor in factors.items():
        out[name] = (out[name] * factor).astype(out[name].dtype)
    return out
```

```python
from contextlib import ExitStack

import concourse.bass as bass
from concourse import mybir

ALU = mybir.AluOpType
ACT = mybir.ActivationFunctionType
AX = mybir.AxisListType
F32 = mybir.dt.float32
F16 = mybir.dt.float16
I32 = mybir.dt.int32

P = 128
CHUNK = 512
TILES = CHUNK // P
PAIR = 2 * P
BANK = 512
HEADS = 16
EPS = 1e-5
FFN_SCALE = 1.0 / 127.0
EXPONENT = 0x7F800000
EXACT_INT = 2048.0

X_UP = 2.0 ** 10
W_UP = 2.0 ** 14
H_DOWN = 2.0 ** -20
TINY = 2.0 ** -96


def build(nc, x, wqT, wkT, wvT, wpT, bp, conv_w, conv_b, wgT, wuT, wdT, out):
    NB, S, D = x.shape
    HID = wgT.shape[1]
    KT = D // P
    J = HID // P
    HPB = HEADS // KT
    HD = D // HEADS
    CB = S // CHUNK
    AW = P + HPB
    VW = P + 1
    assert CB == 2 and KT == 2 and TILES == 4 and KT * D == BANK and KT * PAIR == BANK

    x_v = x.rearrange("b (c i p) d -> (b c) p i d", c=CB, p=P)
    out_v = out.rearrange("b (c i p) d -> (b c) p i d", c=CB, p=P)

    def at(b, c, per_step, k):
        return b * (CB * per_step) + (c * per_step + k)

    with ExitStack() as ctx:
        def sb(name, shape, dt=F32):
            return ctx.enter_context(nc.sbuf_tensor(name, shape, dt))

        def sem(name):
            return ctx.enter_context(nc.semaphore(name))

        names = ["q", "k", "v", "p"]
        w_raw = {n: sb(f"w{n}_raw", [P, KT, D]) for n in names}
        ffn_raw = {n: sb(f"w{n}_int", [P, HID * D // P], I32) for n in "gud"}
        kv_w = [sb(f"kv_w{h}", [P, KT, 2 * D], F16) for h in "hl"]
        q_w = [sb(f"q_w{h}", [P, KT, D], F16) for h in "hl"]
        p_w = [sb(f"p_w{h}", [P, KT, D], F16) for h in "hl"]
        g_w = [sb(f"g_w{h}", [P, KT, HID], F16) for h in "hl"]
        u_w = [sb(f"u_w{h}", [P, KT, HID], F16) for h in "hl"]
        d_w = [sb(f"d_w{h}", [P, J, D], F16) for h in "hl"]
        cw_raw = sb("cw_raw", [P, KT, 3])
        cb_raw = sb("cb_raw", [P, KT])
        cw = sb("cw", [P, KT, 3])
        cb = sb("cb", [P, KT])
        bp_sb = sb("bp_sb", [P, D])
        ident = sb("ident", [P, P])
        head_mask = sb("head_mask", [P, P])
        half = sb("half", [P, TILES])

        A_COLS = {"k": 0, "v": 1, "q": 2, "p": 3, "cw": 4, "cb": 5}
        F_COLS = {"g": 0, "u": 1, "d": 2}
        EARLY = 2
        NA, NF = len(A_COLS), len(F_COLS)
        a_max = sb("a_max", [P, NA]); a_all = sb("a_all", [P, NA])
        a_pow = sb("a_pow", [P, NA]); a_up = sb("a_up", [P, NA])
        f_max = sb("f_max", [P, NF]); f_all = sb("f_all", [P, NF])
        f_pow = sb("f_pow", [P, NF]); f_up = sb("f_up", [P, NF])
        y_sc = sb("y_sc", [P, 11])
        f_sc = sb("f_sc", [P, 6])
        wide = sb("wide", [P, NF]); wide_any = sb("wide_any", [P, 1])

        def a_col(of, name):
            return of[:, A_COLS[name]:A_COLS[name] + 1]

        q_down, k_down = y_sc[:, 0:1], y_sc[:, 1:2]
        y_up, tap_up, attn_to_y, y_down = y_sc[:, 2:3], y_sc[:, 3:4], y_sc[:, 4:5], y_sc[:, 5:6]
        silu_in, h_mul, f_down = f_sc[:, 0:1], f_sc[:, 1:2], f_sc[:, 2:3]
        q_flip, k_flip = y_sc[:, 9:10], y_sc[:, 10:11]

        x_in = sb("x_in", [P, CB, TILES, D])
        bn_raw = sb("bn_raw", [P, CB, TILES, 6])
        ln_tmp = sb("ln_tmp", [P, 5, TILES])
        neg_mean = sb("neg_mean", [P, CB, TILES])
        var_eps = sb("var_eps", [P, CB, TILES])
        rstd = sb("rstd", [P, CB, TILES])
        xn = sb("xn", [P, TILES, D])
        xb = sb("xb", [P, CB, TILES, D])
        xT = sb("xT", [P, CB, KT, CHUNK + 2])
        xh = sb("xh", [P, CB, KT, CHUNK], F16)
        xl = sb("xl", [P, CB, KT, CHUNK], F16)
        k_neg = sb("k_neg", [P, 2, 2, D])
        k_exp = sb("k_exp", [P, 2, 2, D])
        k_relu = sb("k_relu", [P, 2, 2, D])
        k_sb = sb("k_sb", [P, TILES, D])
        v_sb = sb("v_sb", [P, TILES, KT, VW])
        q_neg = sb("q_neg", [P, KT, CHUNK])
        q_exp = sb("q_exp", [P, KT, CHUNK])
        q_relu = sb("q_relu", [P, KT, CHUNK])
        q_sb = sb("q_sb", [P, CB, KT, CHUNK])
        state = sb("state", [P, KT, AW])
        den = sb("den", [P, TILES, KT, HPB])
        rden = sb("rden", [P, TILES, KT, HPB])
        attn = sb("attn", [P, TILES, D])
        local = sb("local", [P, KT, S])
        y = sb("y", [P, KT, CHUNK])
        yh = sb("yh", [P, KT, CHUNK], F16)
        yl = sb("yl", [P, KT, CHUNK], F16)
        act_g = sb("act_g", [P, 2, CHUNK])
        hid = sb("hid", [P, 2, CHUNK])
        hh = sb("hh", [P, J, CHUNK], F16)
        hl = sb("hl", [P, J, CHUNK], F16)
        res = sb("res", [P, CB, TILES, D])
        out_sb = sb("out_sb", [P, CB, TILES, D])

        ps = ctx.enter_context(nc.psum_tensor("ps", [P, 8, BANK], F32))
        def gate_bank(j):
            return 2 * ((j + 1) % 2)
        RING = [4, 5, 7]
        STATE = 6
        QKV = [RING[i % 3] for i in range(4)]
        YT = [RING[4 % 3], RING[5 % 3]]
        WP = [RING[6 % 3], RING[7 % 3]]
        XT = [RING[8 % 3], RING[9 % 3]]
        DOWN = [RING[10 % 3], RING[11 % 3]]

        def halves(bank):
            return ps[:, bank, :].rearrange("p (k n) -> p k n", k=2)

        w_in = {n: sem(f"w{n}_loaded") for n in ["q", "k", "v", "p", "g", "u", "d"]}
        small_in = sem("small_loaded")
        consts = sem("consts_made")
        ones_made = sem("ones_made")
        kv_maxed, kv_reduced, kv_scaled = sem("kv_maxed"), sem("kv_reduced"), sem("kv_scaled")
        a_maxed, a_reduced, a_scaled = sem("a_maxed"), sem("a_reduced"), sem("a_scaled")
        f_maxed, f_reduced, f_scaled = sem("f_maxed"), sem("f_reduced"), sem("f_scaled")
        small_op = sem("scale_steps")
        kv_hi, kv_lo, qp_hi, qp_lo = sem("kv_hi"), sem("kv_lo"), sem("qp_hi"), sem("qp_lo")
        ffn_hi, ffn_lo = sem("ffn_hi"), sem("ffn_lo")
        wide_seen = sem("wide_seen")
        taps_made = sem("taps_made")
        x_loaded = [sem(f"x_loaded{c}") for c in range(CB)]
        out_stored = [sem(f"out_stored{c}") for c in range(CB)]
        bn_seen, bn_merged, ln_ready = sem("bn_seen"), sem("bn_merged"), sem("ln_ready")
        bn_squared, bn_var = sem("bn_squared"), sem("bn_var")
        rstd_ready, xn_ready, xb_ready = sem("rstd_ready"), sem("xn_ready"), sem("xb_ready")
        xT_done, xT_ready, xl_ready = sem("xT_done"), sem("xT_ready"), sem("xl_ready")
        kv_done, k_parts, v_ready, k_ready = sem("kv_done"), sem("k_parts"), sem("v_ready"), sem("k_ready")
        acc_done, state_ready = sem("acc_done"), sem("state_ready")
        q_done, q_parts, q_ready = sem("q_done"), sem("q_parts"), sem("q_ready")
        k_flipped, q_flipped, q_read = sem("k_flipped"), sem("q_flipped"), sem("q_read")
        qkv_done, den_kept, den_inv, attn_ready = sem("qkv_done"), sem("den_kept"), sem("den_inv"), sem("attn_ready")
        yT_done, y_ready, yh_ready, yl_ready = sem("yT_done"), sem("y_ready"), sem("yh_ready"), sem("yl_ready")
        wp_done, out_ready = sem("wp_done"), sem("out_ready")
        gu_done, silu_ready, hid_ready = sem("gu_done"), sem("silu_ready"), sem("hid_ready")
        hh_ready, hl_ready, down_done, res_ready = sem("hh_ready"), sem("hl_ready"), sem("down_done"), sem("res_ready")
        mid_tap, left_tap, conv_done = sem("mid_tap"), sem("left_tap"), sem("conv_done")

        block = ctx.enter_context(nc.Block())

        def run(eng, step):
            step(0, 0, False, True, True)
            step(0, 1, False, True, True)
            with eng.Fori(1, NB - 1) as b:
                step(b, 0, True, True, True)
                step(b, 1, True, True, True)
            step(NB - 1, 0, True, True, True)
            step(NB - 1, 1, True, True, False)
            step(NB, 0, True, False, False)
            step(NB, 1, True, False, False)

        @block.sync
        def _(sp):
            sp.dma_start(x_in[:, 0, :, :], x_v[0]).then_inc(x_loaded[0], 16)
            sp.dma_start(cw_raw[:, :, :], conv_w.rearrange("(k p) t -> p k t", p=P)).then_inc(small_in, 16)
            sp.dma_start(cb_raw[:, :], conv_b.rearrange("(k p) -> p k", p=P),
                         allow_slow_non_contiguous=True).then_inc(small_in, 16)
            for n, w in (("q", wqT), ("p", wpT)):
                sp.dma_start(w_raw[n][:, :, :], w.rearrange("(k p) n -> p k n", p=P)).then_inc(w_in[n], 16)
            sp.dma_start(bp_sb[:, :], bp.rearrange("(o n) -> o n", o=1).broadcast_to([P, D])).then_inc(small_in, 16)
            for n, w in (("g", wgT), ("u", wuT), ("d", wdT)):
                sp.dma_start(ffn_raw[n][:, :].rearrange("p (k n) -> p k n", n=w.shape[1]),
                             w.rearrange("(k p) n -> p k n", p=P)).then_inc(w_in[n], 16)
                if n == "g":
                    sp.dma_start(x_in[:, 1, :, :], x_v[1]).then_inc(x_loaded[1], 16)

            def step(b, c, attend, feed, ahead):
                if attend:
                    sp.wait_ge(out_ready, at(b - 1, c, 2, 2))
                    sp.dma_start(out_v[CB * b + (c - CB)], out_sb[:, c, :, :]).then_inc(out_stored[c], 16)
                if feed and not (isinstance(b, int) and b == NB - 1):
                    if isinstance(b, int) and b == 0 and c == 0:
                        sp.wait_ge(xb_ready, 1)
                    sp.wait_ge(xn_ready, at(b, c, 2, 2))
                    sp.dma_start(x_in[:, c, :, :], x_v[CB * b + (c + CB)]).then_inc(x_loaded[c], 16)

            run(sp, step)
            for c in range(CB):
                sp.wait_ge(out_stored[c], 16 * NB)

        @block.gpsimd
        def _(pool):
            def add_bias(b, c):
                nc.gpsimd.tensor_tensor(xb[:, c, :, :], x_in[:, c, :, :],
                                        bp_sb[:, :].unsqueeze(1).broadcast_to([P, TILES, D]),
                                        ALU.add).then_inc(xb_ready, 1)

            def normalise(c, i):
                return nc.gpsimd.tensor_scalar(xn[:, i, :], x_in[:, c, i, :], neg_mean[:, c, i:i + 1],
                                               rstd[:, c, i:i + 1], ALU.add, ALU.mult)

            def layernorm(b, c):
                pool.wait_ge(ln_ready, at(b, c, 1, 1))
                nc.gpsimd.tensor_tensor(rstd[:, c, :], var_eps[:, c, :], half[:, :], ALU.pow).then_inc(rstd_ready, 1)
                pool.wait_ge(rstd_ready, at(b, c, 1, 1))
                pool.wait_ge(xT_done, at(b, c - 1, 2, 2))
                add_bias(b, c)
                for i in range(TILES):
                    ins = normalise(c, i)
                    if i % 2 == 1:
                        ins.then_inc(xn_ready, 1)

            def across(dst, src):
                return nc.gpsimd.partition_all_reduce(dst, src, P, bass.bass_isa.ReduceOp.max)

            nc.gpsimd.memset(half[:, :], -0.5).then_inc(consts, 1)
            nc.gpsimd.memset(ident[:, :], 0.0).then_inc(consts, 1)
            nc.gpsimd.memset(head_mask[:, :], 1.0).then_inc(consts, 1)
            nc.gpsimd.memset(v_sb[:, :, :, P:VW], 1.0).then_inc(ones_made, 1)
            nc.gpsimd.memset(xT[:, 0, :, 0:1], 0.0).then_inc(ones_made, 1)
            nc.gpsimd.memset(xT[:, 1, :, CHUNK + 1:CHUNK + 2], 0.0).then_inc(ones_made, 1)
            pool.wait_ge(consts, 3)
            nc.gpsimd.affine_select(out=ident[:, :], in_=ident[:, :], compare_op=ALU.not_equal, fill=1.0,
                                    base=0, pattern=[[-1, P]], channel_multiplier=1).then_inc(consts, 1)
            hm = head_mask[:, :].rearrange("p (h e) -> p h e", h=HPB)
            nc.gpsimd.affine_select(out=hm, in_=hm, compare_op=ALU.is_ge, fill=0.0, base=0,
                                    pattern=[[-HD, HPB], [0, HD]], channel_multiplier=1).then_inc(consts, 1)
            pool.wait_ge(consts, 5)
            nc.gpsimd.affine_select(out=hm, in_=hm, compare_op=ALU.is_ge, fill=0.0, base=HD - 1,
                                    pattern=[[HD, HPB], [0, HD]], channel_multiplier=-1).then_inc(consts, 1)
            pool.wait_ge(ln_ready, 1)
            nc.gpsimd.tensor_tensor(rstd[:, 0, :], var_eps[:, 0, :], half[:, :], ALU.pow).then_inc(rstd_ready, 1)
            pool.wait_ge(rstd_ready, 1)
            normalise(0, 0)
            normalise(0, 1).then_inc(xn_ready, 1)
            pool.wait_ge(kv_maxed, EARLY)
            across(a_all[:, 0:EARLY], a_max[:, 0:EARLY]).then_inc(kv_reduced, 1)
            normalise(0, 2)
            normalise(0, 3).then_inc(xn_ready, 1)
            pool.wait_ge(a_maxed, NA - EARLY)
            across(a_all[:, EARLY:NA], a_max[:, EARLY:NA]).then_inc(a_reduced, 1)
            pool.wait_ge(small_in, 48)
            add_bias(0, 0)
            pool.wait_ge(f_maxed, NF)
            across(f_all[:, :], f_max[:, :]).then_inc(f_reduced, 1)

            def step(b, c, attend, feed, ahead):
                if ahead:
                    layernorm(*((b, 1) if c == 0 else (b + 1, 0)))

            run(pool, step)

        @block.scalar
        def _(act):
            def transposed(b, c, first):
                for p in range(2):
                    act.wait_ge(xT_done, at(b, c, 2, p + 1))
                    src = halves(XT[p])
                    if p == 0 and not (isinstance(b, int) and b == 0):
                        act.wait_ge(conv_done, at(b, c, KT, -KT))
                    nc.scalar.activation(xT[:, c, :, 1 + p * PAIR:1 + (p + 1) * PAIR], src, ACT.Copy)
                    if c == 1 and p == 0:
                        nc.scalar.activation(xT[:, 0, :, CHUNK + 1:CHUNK + 2], src[:, :, 0:1], ACT.Copy)
                        act.wait_ge(xT_ready, at(b, 0, 2, 2))
                        nc.scalar.activation(xT[:, 1, :, 0:1], xT[:, 0, :, CHUNK:CHUNK + 1], ACT.Copy)
                    nc.scalar.activation(xh[:, c, :, p * PAIR:(p + 1) * PAIR], src, ACT.Copy).then_inc(xT_ready, 1)

            for n, w in (("k", wkT), ("v", wvT)):
                act.dma_start(w_raw[n][:, :, :], w.rearrange("(k p) n -> p k n", p=P)).then_inc(w_in[n], 16)
            nc.scalar.preload_act_table(ACT.Exp)

            def high(dst, src, scale, done):
                nc.scalar.activation(dst, src, ACT.Copy, scale=scale).then_inc(done, 1)

            act.wait_ge(kv_scaled, 1)
            high(kv_w[0][:, :, 0:D], w_raw["k"][:, :, :], a_col(a_up, "k"), kv_hi)
            high(kv_w[0][:, :, D:2 * D], w_raw["v"][:, :, :], a_col(a_up, "v"), kv_hi)
            transposed(0, 0, True)
            act.wait_ge(a_scaled, 1)
            high(q_w[0][:, :, :], w_raw["q"][:, :, :], a_col(a_up, "q"), qp_hi)
            high(p_w[0][:, :, :], w_raw["p"][:, :, :], a_col(a_up, "p"), qp_hi)

            def step(b, c, attend, feed, ahead):
                past = not (isinstance(b, int) and b == 0 and c == 0)

                def middle_tap(k):
                    pb, pc = (b, 0) if c == 1 else (b - 1, 1)
                    if k == 0:
                        if feed:
                            act.wait_ge(xT_ready, at(b, c, 2, 1))
                        if not (isinstance(pb, int) and pb == 0):
                            act.wait_ge(y_ready, at(pb - 1, pc, 2, 2))
                        elif pc == 0:
                            act.wait_ge(taps_made, 2)
                    nc.scalar.activation(local[:, k, pc * CHUNK:(pc + 1) * CHUNK], xT[:, pc, k, 1:1 + CHUNK],
                                         ACT.Identity, scale=cw[:, k, 1:2], bias=cb[:, k:k + 1]).then_inc(mid_tap, 1)

                convolve = past and not (isinstance(b, int) and b == NB and c == 1)
                if convolve:
                    middle_tap(0)
                    middle_tap(1)
                if feed:
                    for p in range(2):
                        bank = 2 * p
                        act.wait_ge(kv_done, at(b, c, 2, p + 1))
                        if past:
                            act.wait_ge(k_ready, at(b, c - 1, 2, p + 1))
                        nc.scalar.activation(k_neg[:, p, :, :], ps[:, bank:bank + 2, 0:D], ACT.Relu,
                                             scale=k_flip).then_inc(k_flipped, 1)
                        nc.scalar.activation(k_relu[:, p, :, :], ps[:, bank:bank + 2, 0:D], ACT.Relu,
                                             scale=k_down)
                        if past:
                            act.wait_ge(acc_done, at(b, c - 1, 2, p + 1))
                        elif p == 0:
                            act.wait_ge(ones_made, 3)
                        for i in range(2):
                            ins = nc.scalar.activation(v_sb[:, 2 * p + i, :, 0:P],
                                                       ps[:, bank + i, D:2 * D].rearrange("p (k n) -> p k n", k=KT),
                                                       ACT.Copy)
                        ins.then_inc(v_ready, 1)
                        act.wait_ge(k_flipped, at(b, c, 2, p + 1))
                        nc.scalar.activation(k_exp[:, p, :, :], k_neg[:, p, :, :], ACT.Exp,
                                             scale=-1.0).then_inc(k_parts, 1)
                    act.wait_ge(q_done, at(b, c, 1, 1))
                    if past:
                        act.wait_ge(q_ready, at(b, c - 1, 1, 1))
                    nc.scalar.activation(q_neg[:, :, :], ps[:, 0:2, :], ACT.Relu, scale=q_flip).then_inc(q_flipped, 1)
                    nc.scalar.activation(q_relu[:, :, :], ps[:, 0:2, :], ACT.Relu, scale=q_down).then_inc(q_read, 1)
                    act.wait_ge(q_flipped, at(b, c, 1, 1))
                    nc.scalar.activation(q_exp[:, :, :], q_neg[:, :, :], ACT.Exp, scale=-1.0).then_inc(q_parts, 1)

                def y_high(p):
                    cols = slice(p * PAIR, (p + 1) * PAIR)
                    act.wait_ge(y_ready, at(b - 1, c, 2, p + 1))
                    nc.scalar.activation(yh[:, :, cols], y[:, :, cols], ACT.Copy).then_inc(yh_ready, 1)

                def silu(j):
                    act.wait_ge(gu_done, at(b, c, J, j + 1))
                    if past or j >= 2:
                        act.wait_ge(hid_ready, at(b, c, J, j - 1))
                    nc.scalar.activation(act_g[:, j % 2, :], ps[:, gate_bank(j), :], ACT.Silu,
                                         scale=silu_in).then_inc(silu_ready, 1)

                def hidden_high(j):
                    act.wait_ge(hid_ready, at(b, c, J, j + 1))
                    if past and j == 0:
                        act.wait_ge(down_done, at(b, c - 1, 2, 2))
                    nc.scalar.activation(hh[:, j, :], hid[:, j % 2, :], ACT.Copy).then_inc(hh_ready, 1)

                if attend:
                    y_high(0)
                    y_high(1)
                if feed:
                    if isinstance(b, int) and b == 0 and c == 0:
                        act.wait_ge(f_scaled, 1)
                        high(d_w[0][:, :, :], ffn_raw["d"][:, :].rearrange("p (k n) -> p k n", k=J), f_up[:, 2:3], ffn_hi)
                    nc.scalar.preload_act_table(ACT.Silu)
                    for j in range(J):
                        silu(j)
                        if j >= 1:
                            hidden_high(j - 1)
                    hidden_high(J - 1)
                    nc.scalar.preload_act_table(ACT.Exp)
                if ahead:
                    transposed(*((b, 1) if c == 0 else (b + 1, 0)), False)

            run(act, step)

        @block.vector
        def _(dve):
            def stats(b, c):
                dve.wait_ge(x_loaded[c], (b + 1) * 16)
                for i in range(TILES):
                    nc.vector.bn_stats(bn_raw[:, c, i, :], x_in[:, c, i, :]).then_inc(bn_seen, 1)
                even, odd = bn_raw[:, c, :, 0:3], bn_raw[:, c, :, 3:6]
                total, apart, spread, square, var = (ln_tmp[:, n, :] for n in range(5))
                dve.wait_ge(bn_seen, at(b, c, TILES, TILES))
                nc.vector.tensor_tensor(apart, even[:, :, 1], odd[:, :, 1], ALU.subtract)
                nc.vector.tensor_tensor(spread, even[:, :, 2], odd[:, :, 2], ALU.add)
                nc.vector.tensor_tensor(total, even[:, :, 1], odd[:, :, 1], ALU.add).then_inc(bn_merged, 1)
                dve.wait_ge(bn_merged, at(b, c, 1, 1))
                nc.vector.tensor_scalar(neg_mean[:, c, :], total, -0.5, None, ALU.mult)
                nc.vector.scalar_tensor_tensor(out=square, in0=apart, scalar=0.25, in1=apart, op0=ALU.mult,
                                               op1=ALU.mult).then_inc(bn_squared, 1)
                dve.wait_ge(bn_squared, at(b, c, 1, 1))
                nc.vector.scalar_tensor_tensor(out=var, in0=spread, scalar=1.0 / D, in1=square, op0=ALU.mult,
                                               op1=ALU.add).then_inc(bn_var, 1)
                dve.wait_ge(bn_var, at(b, c, 1, 1))
                nc.vector.tensor_scalar(var_eps[:, c, :], var, EPS, X_UP ** -2,
                                        ALU.add, ALU.mult).then_inc(ln_ready, 1)

            def x_low(b, c):
                for p in range(2):
                    cols = slice(p * PAIR, (p + 1) * PAIR)
                    dve.wait_ge(xT_ready, at(b, c, 2, p + 1))
                    nc.vector.tensor_tensor(xl[:, c, :, cols], xT[:, c, :, 1 + p * PAIR:1 + (p + 1) * PAIR], xh[:, c, :, cols],
                                            ALU.subtract).then_inc(xl_ready, 1)

            ops = [0]

            def scale_op(ins):
                ops[0] += 1
                ins.then_inc(small_op, 1)
                dve.wait_ge(small_op, ops[0])

            def powers(pow_, up, largest):
                scale_op(nc.vector.tensor_scalar(pow_, largest, TINY, None, ALU.max))
                scale_op(nc.vector.tensor_scalar(pow_.bitcast(I32), pow_.bitcast(I32), EXPONENT, None,
                                                 ALU.bitwise_and))
                scale_op(nc.vector.reciprocal(up, pow_))
                scale_op(nc.vector.tensor_scalar(up, up, W_UP, None, ALU.mult))

            def largest(dst, src, dims):
                return nc.vector.tensor_reduce(dst, src, dims, ALU.max, apply_absolute_value=True)

            def low(dst, src, scale, hi, halved, n, done):
                dve.wait_ge(halved, n)
                nc.vector.scalar_tensor_tensor(out=dst, in0=src, scalar=scale, in1=hi, op0=ALU.mult,
                                               op1=ALU.subtract).then_inc(done, 1)

            def attention_maxima(names, done):
                for n in names:
                    dve.wait_ge(w_in[n], 16)
                    largest(a_col(a_max, n), w_raw[n][:, :, :], AX.XY).then_inc(done, 1)

            def ffn_maximum(n):
                dve.wait_ge(w_in[n], 16)
                largest(f_max[:, F_COLS[n]:F_COLS[n] + 1], ffn_raw[n][:, :], AX.X).then_inc(f_maxed, 1)

            stats(0, 0)
            attention_maxima(["k", "v"], kv_maxed)
            attention_maxima(["q", "p"], a_maxed)
            dve.wait_ge(small_in, 48)
            largest(a_col(a_max, "cw"), cw_raw[:, :, :], AX.XY).then_inc(a_maxed, 1)
            largest(a_col(a_max, "cb"), cb_raw[:, :], AX.X).then_inc(a_maxed, 1)
            dve.wait_ge(kv_reduced, 1)
            powers(a_pow[:, 0:EARLY], a_up[:, 0:EARLY], a_all[:, 0:EARLY])
            nc.vector.tensor_scalar(k_flip, a_col(a_pow, "k"), -1.0 / (X_UP * W_UP), None, ALU.mult)
            nc.vector.tensor_scalar(k_down, a_col(a_pow, "k"), 1.0 / (X_UP * W_UP), None,
                                    ALU.mult).then_inc(kv_scaled, 1)
            low(kv_w[1][:, :, 0:D], w_raw["k"][:, :, :], a_col(a_up, "k"), kv_w[0][:, :, 0:D], kv_hi, 1, kv_lo)
            low(kv_w[1][:, :, D:2 * D], w_raw["v"][:, :, :], a_col(a_up, "v"), kv_w[0][:, :, D:2 * D], kv_hi, 2, kv_lo)
            x_low(0, 0)
            dve.wait_ge(a_reduced, 1)
            powers(a_pow[:, EARLY:NA], a_up[:, EARLY:NA], a_all[:, EARLY:NA])
            nc.vector.tensor_scalar(q_flip, a_col(a_pow, "q"), -1.0 / (X_UP * W_UP), None, ALU.mult)
            nc.vector.tensor_scalar(q_down, a_col(a_pow, "q"), 1.0 / (X_UP * W_UP), None, ALU.mult).then_inc(a_scaled, 1)
            ffn_maximum("g")
            low(q_w[1][:, :, :], w_raw["q"][:, :, :], a_col(a_up, "q"), q_w[0][:, :, :], qp_hi, 1, qp_lo)
            low(p_w[1][:, :, :], w_raw["p"][:, :, :], a_col(a_up, "p"), p_w[0][:, :, :], qp_hi, 2, qp_lo)
            ffn_maximum("u")
            ffn_maximum("d")

            def ffn_scales():
                dve.wait_ge(f_reduced, 1)
                powers(f_pow[:, :], f_up[:, :], f_all[:, :])
                nc.vector.tensor_scalar(silu_in, f_pow[:, 0:1], FFN_SCALE / (X_UP * W_UP), None, ALU.mult)
                nc.vector.tensor_scalar(h_mul, f_up[:, 0:1], H_DOWN / W_UP, None, ALU.mult)
                nc.vector.tensor_scalar(wide[:, :], f_all[:, :], EXACT_INT, None, ALU.is_gt)
                scale_op(nc.vector.scalar_tensor_tensor(out=f_sc[:, 3:4], in0=f_pow[:, 0:1],
                                                        scalar=FFN_SCALE ** 2 / (H_DOWN * X_UP * W_UP * W_UP),
                                                        in1=f_pow[:, 1:2], op0=ALU.mult, op1=ALU.mult))
                nc.vector.tensor_reduce(wide_any[:, :], wide[:, :], AX.X, ALU.max).then_inc(wide_seen, 1)
                nc.vector.tensor_tensor(f_down, f_sc[:, 3:4], f_pow[:, 2:3], ALU.mult).then_inc(f_scaled, 1)

            def ffn_high(n, w):
                i = F_COLS[n]
                nc.vector.tensor_scalar(w[0][:, :, :], ffn_raw[n][:, :].rearrange("p (k n) -> p k n", k=KT),
                                        f_up[:, i:i + 1], None, ALU.mult).then_inc(ffn_hi, 1)

            def ffn_low_halves():
                dve.wait_ge(wide_seen, 1)
                any_wide = dve.value_load(wide_any[0:1, 0:1].bitcast(I32))
                with dve.If(any_wide):
                    for i, (n, w, k) in enumerate((("g", g_w, KT), ("u", u_w, KT), ("d", d_w, J))):
                        low(w[1][:, :, :], ffn_raw[n][:, :].rearrange("p (k n) -> p k n", k=k), f_up[:, i:i + 1],
                            w[0][:, :, :], ffn_hi, NF, ffn_lo)

            def attention_scales():
                t = [y_sc[:, 6:7], y_sc[:, 7:8], y_sc[:, 8:9]]
                scale_op(nc.vector.tensor_scalar(t[0], a_col(a_pow, "v"), 512.0, None, ALU.mult))
                scale_op(nc.vector.scalar_tensor_tensor(out=t[1], in0=a_col(a_pow, "cw"), scalar=128.0, in1=t[0],
                                                        op0=ALU.mult, op1=ALU.add))
                scale_op(nc.vector.scalar_tensor_tensor(out=t[0], in0=a_col(a_pow, "cb"), scalar=2.0, in1=t[1],
                                                        op0=ALU.mult, op1=ALU.add))
                scale_op(nc.vector.tensor_scalar(t[1].bitcast(I32), t[0].bitcast(I32), EXPONENT, None,
                                                 ALU.bitwise_and))
                scale_op(nc.vector.reciprocal(t[2], t[1]))
                scale_op(nc.vector.tensor_scalar(y_up, t[2], W_UP, None, ALU.mult))
                nc.vector.tensor_scalar(cb[:, :], cb_raw[:, :], y_up, None, ALU.mult).then_inc(taps_made, 1)
                nc.vector.scalar_tensor_tensor(out=attn_to_y, in0=a_col(a_pow, "v"), scalar=1.0 / (X_UP * W_UP),
                                               in1=y_up, op0=ALU.mult, op1=ALU.mult)
                nc.vector.scalar_tensor_tensor(out=y_down, in0=a_col(a_pow, "p"), scalar=W_UP ** -2, in1=t[1],
                                               op0=ALU.mult, op1=ALU.mult)
                scale_op(nc.vector.tensor_scalar(tap_up, y_up, 1.0 / X_UP, None, ALU.mult))
                nc.vector.tensor_scalar(cw[:, :, :], cw_raw[:, :, :], tap_up, None, ALU.mult).then_inc(taps_made, 1)

            def step(b, c, attend, feed, ahead):
                past = not (isinstance(b, int) and b == 0 and c == 0)
                nb, ncx = (b, 1) if c == 0 else (b + 1, 0)

                def normalise(p):
                    tiles = (2 * p, 2 * p + 1)
                    src = {i: ps[:, QKV[i], 0:KT * AW].rearrange("p (k n) -> p k n", k=KT) for i in tiles}
                    for i in tiles:
                        dve.wait_ge(qkv_done, at(b - 1, c, TILES, i + 1))
                        nc.vector.tensor_scalar(den[:, i, :, :], src[i][:, :, P:AW], 1e-6, None,
                                                ALU.max).then_inc(den_kept, 1)
                    for i in tiles:
                        dve.wait_ge(den_kept, at(b - 1, c, TILES, i + 1))
                        nc.vector.reciprocal(rden[:, i, :, :], den[:, i, :, :]).then_inc(den_inv, 1)
                    for i in tiles:
                        dve.wait_ge(den_inv, at(b - 1, c, TILES, i + 1))
                        nc.vector.tensor_tensor(attn[:, i, :].rearrange("p (k h e) -> p k h e", k=KT, h=HPB),
                                                src[i][:, :, 0:P].rearrange("p k (h e) -> p k h e", h=HPB),
                                                rden[:, i, :, :].unsqueeze(3).broadcast_to([P, KT, HPB, HD]),
                                                ALU.mult).then_inc(attn_ready, 1)

                def put_k(p):
                    dve.wait_ge(k_parts, at(b, c, 2, p + 1))
                    if past:
                        dve.wait_ge(acc_done, at(b, c - 1, 2, p + 1))
                    nc.vector.tensor_tensor(k_sb[:, 2 * p:2 * p + 2, :], k_exp[:, p, :, :], k_relu[:, p, :, :],
                                            ALU.add).then_inc(k_ready, 1)

                def put_y(p):
                    cols = slice(p * PAIR, (p + 1) * PAIR)
                    dve.wait_ge(yT_done, at(b - 1, c, 2, p + 1))
                    if p == 0:
                        dve.wait_ge(conv_done, at(b - 1, c, KT, KT))
                    first_y = isinstance(b, int) and b == 1 and c == 0
                    if not first_y:
                        dve.wait_ge(yl_ready, at(b - 1, c, 2, p - 1))
                        dve.wait_ge(wp_done, at(b - 1, c, 2, p - 1))
                    nc.vector.scalar_tensor_tensor(out=y[:, :, cols], in0=halves(YT[p]), scalar=attn_to_y,
                                                   in1=local[:, :, c * CHUNK + p * PAIR:c * CHUNK + (p + 1) * PAIR],
                                                   op0=ALU.mult, op1=ALU.add).then_inc(y_ready, 1)

                def y_low(p):
                    cols = slice(p * PAIR, (p + 1) * PAIR)
                    dve.wait_ge(yh_ready, at(b - 1, c, 2, p + 1))
                    nc.vector.tensor_tensor(yl[:, :, cols], y[:, :, cols], yh[:, :, cols],
                                            ALU.subtract).then_inc(yl_ready, 1)

                def hidden(j):
                    dve.wait_ge(silu_ready, at(b, c, J, j + 1))
                    if past or j >= 2:
                        dve.wait_ge(hl_ready, at(b, c, J, j - 1))
                    nc.vector.scalar_tensor_tensor(out=hid[:, j % 2, :], in0=act_g[:, j % 2, :], scalar=h_mul,
                                                   in1=ps[:, gate_bank(j) + 1, :], op0=ALU.mult,
                                                   op1=ALU.mult).then_inc(hid_ready, 1)

                def hidden_low(j):
                    dve.wait_ge(hh_ready, at(b, c, J, j + 1))
                    nc.vector.tensor_tensor(hl[:, j, :], hid[:, j % 2, :], hh[:, j, :],
                                            ALU.subtract).then_inc(hl_ready, 1)

                def tap(k, side):
                    pb, pc = (b, 0) if c == 1 else (b - 1, 1)
                    done, before = (left_tap, mid_tap) if side == 0 else (conv_done, left_tap)
                    dve.wait_ge(before, at(pb, pc, KT, k + 1))
                    here = local[:, k, pc * CHUNK:(pc + 1) * CHUNK]
                    nc.vector.scalar_tensor_tensor(out=here, in0=xT[:, pc, k, side:side + CHUNK],
                                                   scalar=cw[:, k, side:side + 1], in1=here,
                                                   op0=ALU.mult, op1=ALU.add).then_inc(done, 1)

                def put_state():
                    dve.wait_ge(acc_done, at(b, c, 2, 2))
                    acc = halves(STATE)
                    for k in range(KT):
                        nc.vector.tensor_tensor(state[:, k, 0:P], acc[:, k, 0:P], head_mask[:, :], ALU.mult)
                        ins = nc.vector.tensor_scalar(state[:, k, P:AW], head_mask[:, 0:P:HD],
                                                      acc[:, k, P:P + 1], None, ALU.mult)
                    ins.then_inc(state_ready, 1)

                def output(p):
                    dve.wait_ge(wp_done, at(b - 1, c, 2, p + 1))
                    if not (isinstance(b, int) and b == 1):
                        dve.wait_ge(out_stored[c], (b - 1) * 16)
                    nc.vector.scalar_tensor_tensor(out=out_sb[:, c, 2 * p:2 * p + 2, :], in0=halves(WP[p]),
                                                   scalar=y_down, in1=res[:, c, 2 * p:2 * p + 2, :],
                                                   op0=ALU.mult, op1=ALU.add).then_inc(out_ready, 1)

                convolve = past and not (isinstance(b, int) and b == NB and c == 1)
                if convolve:
                    tap(0, 0)
                    tap(1, 0)
                if attend:
                    normalise(0)
                if not past:
                    ffn_scales()
                    ffn_high("g", g_w)
                if feed:
                    put_k(0)
                if not past:
                    ffn_high("u", u_w)
                if convolve:
                    tap(0, 2)
                if attend:
                    normalise(1)
                if convolve:
                    tap(1, 2)
                if feed:
                    put_k(1)
                if attend:
                    put_y(0)
                    put_y(1)
                if ahead:
                    stats(nb, ncx)
                if feed:
                    dve.wait_ge(q_parts, at(b, c, 1, 1))
                    nc.vector.tensor_tensor(q_sb[:, c, :, :], q_exp[:, :, :], q_relu[:, :, :],
                                            ALU.add).then_inc(q_ready, 1)
                if attend:
                    y_low(0)
                    y_low(1)
                if not past:
                    ffn_low_halves()
                    attention_scales()
                if feed:
                    for j in range(J):
                        hidden(j)
                        if j >= 1:
                            hidden_low(j - 1)
                        if j == 1 and c == CB - 1:
                            put_state()
                        if j == 3 and attend:
                            output(0)
                elif attend:
                    output(0)
                if attend:
                    output(1)
                if feed:
                    hidden_low(J - 1)
                if ahead:
                    x_low(nb, ncx)
                if feed:
                    for p in range(2):
                        dve.wait_ge(down_done, at(b, c, 2, p + 1))
                        dve.wait_ge(xb_ready, at(b, c, 1, 1))
                        nc.vector.scalar_tensor_tensor(out=res[:, c, 2 * p:2 * p + 2, :], in0=halves(DOWN[p]),
                                                       scalar=f_down, in1=xb[:, c, 2 * p:2 * p + 2, :],
                                                       op0=ALU.mult, op1=ALU.add).then_inc(res_ready, 1)

            step(0, 0, False, True, True)
            step(0, 1, False, True, True)
            step(1, 0, True, True, True)
            step(1, 1, True, True, True)
            with dve.Fori(2, NB - 1) as b:
                step(b, 0, True, True, True)
                step(b, 1, True, True, True)
            step(NB - 1, 0, True, True, True)
            step(NB - 1, 1, True, True, False)
            step(NB, 0, True, False, False)
            step(NB, 1, True, False, False)

        @block.tensor
        def _(pe):
            def transpose_x(b, c, attend, first):
                for p in range(2):
                    pe.wait_ge(xn_ready, at(b, c, 2, p + 1))
                    if not first:
                        if p == 0:
                            if attend:
                                pe.wait_ge(y_ready, at(b - 1, c - 1, 2, 2))
                            elif not (isinstance(b, int) and b == 0 and c == 1):
                                pe.wait_ge(res_ready, at(b, c - 2, 2, 2))
                        else:
                            if attend:
                                pe.wait_ge(out_ready, at(b - 1, c - 1, 2, 1))
                            else:
                                pe.wait_ge(xT_ready, at(b, c - 1, 2, 2))
                    for i in range(2):
                        for k in range(KT):
                            ins = nc.tensor.transpose(ps[:, XT[p], k * PAIR + i * P:k * PAIR + (i + 1) * P],
                                                      xn[:, 2 * p + i, k * P:(k + 1) * P], ident[:, :])
                    ins.then_inc(xT_done, 1)

            def three(dst, stat, mov):
                terms = [(0, 0), (1, 0), (0, 1)]
                for n, (s, m) in enumerate(terms):
                    for k in range(KT):
                        ins = nc.tensor.matmul(dst, stat(s, k), mov(m, k), start=(n == 0 and k == 0),
                                               stop=(n == len(terms) - 1 and k == KT - 1))
                return ins

            pe.wait_ge(consts, 6)
            transpose_x(0, 0, False, True)
            pe.wait_ge(kv_hi, 2)
            pe.wait_ge(kv_lo, 2)

            def step(b, c, attend, feed, ahead, wide=None):
                zero = isinstance(b, int) and b == 0
                past = not (zero and c == 0)
                x2 = [xh, xl]
                y2 = [yh, yl]

                def project_kv(p):
                    pe.wait_ge(xl_ready, at(b, c, 2, p + 1))
                    if past:
                        pe.wait_ge(hid_ready, at(b, c - 1, J, J - p))
                    for i in range(2):
                        t = slice((2 * p + i) * P, (2 * p + i + 1) * P)
                        ins = three(ps[:, 2 * p + i, :], lambda s, k: x2[s][:, c, k, t], lambda m, k: kv_w[m][:, k, :])
                    ins.then_inc(kv_done, 1)

                def accumulate(p):
                    pe.wait_ge(k_ready, at(b, c, 2, p + 1))
                    pe.wait_ge(v_ready, at(b, c, 2, p + 1))
                    if c == 0 and p == 0 and not zero:
                        pe.wait_ge(state_ready, b)
                    for i in (2 * p, 2 * p + 1):
                        for k in range(KT):
                            ins = nc.tensor.matmul(ps[:, STATE, k * D:k * D + VW], k_sb[:, i, k * P:(k + 1) * P],
                                                   v_sb[:, i, k, :], start=(c == 0 and i == 0 and k == 0),
                                                   stop=(c == CB - 1 and i == TILES - 1), skip_group_check=True)
                    ins.then_inc(acc_done, 1)

                def project_q():
                    pe.wait_ge(v_ready, at(b, c, 2, 1))
                    if zero and c == 0:
                        pe.wait_ge(qp_hi, 1)
                        pe.wait_ge(qp_lo, 1)
                    for m in range(KT):
                        ins = three(ps[:, m, :], lambda s, k: q_w[s][:, k, m * P:(m + 1) * P],
                                    lambda s, k: x2[s][:, c, k, :])
                    ins.then_inc(q_done, 1)

                def query(i):
                    if i == 0:
                        pe.wait_ge(state_ready, b)
                        pe.wait_ge(q_ready, at(b - 1, c, 1, 1))
                        if feed:
                            pe.wait_ge(xT_ready, at(b, c, 2, 2))
                        else:
                            pe.wait_ge(out_ready, at(b - 1, c - 1, 2, 1))
                    if i == 1:
                        if feed or c == 0:
                            pe.wait_ge(res_ready, at(b, c - 1, 2, 1))
                        else:
                            pe.wait_ge(out_ready, at(b - 1, c - 1, 2, 2))
                    if i == 2:
                        if feed or c == 0:
                            pe.wait_ge(res_ready, at(b, c - 1, 2, 2))
                        else:
                            pe.wait_ge(y_ready, at(b - 1, c - 1, 2, 2))
                    if i == 3:
                        pe.wait_ge(attn_ready, at(b - 1, c, TILES, 1))
                    for k in range(KT):
                        ins = nc.tensor.matmul(ps[:, QKV[i], k * AW:(k + 1) * AW], q_sb[:, c, k, i * P:(i + 1) * P],
                                               state[:, k, :], start=True, stop=True)
                    ins.then_inc(qkv_done, 1)

                def transpose_attn(p):
                    pe.wait_ge(attn_ready, at(b - 1, c, TILES, 2 * p + 2))
                    for i in range(2):
                        for k in range(KT):
                            ins = nc.tensor.transpose(ps[:, YT[p], k * PAIR + i * P:k * PAIR + (i + 1) * P],
                                                      attn[:, 2 * p + i, k * P:(k + 1) * P], ident[:, :])
                    ins.then_inc(yT_done, 1)

                def project_y(p):
                    if isinstance(b, int) and b == 1 and c == 0 and p == 0:
                        pe.wait_ge(qp_hi, 2)
                        pe.wait_ge(qp_lo, 2)
                    pe.wait_ge(yl_ready, at(b - 1, c, 2, p + 1))
                    for i in range(2):
                        t = slice((2 * p + i) * P, (2 * p + i + 1) * P)
                        ins = three(ps[:, WP[p], i * D:(i + 1) * D], lambda s, k: y2[s][:, k, t],
                                    lambda m, k: p_w[m][:, k, :])
                    ins.then_inc(wp_done, 1)

                def gate_up(j):
                    if j == 0:
                        pe.wait_ge(v_ready, at(b, c, 2, 2))
                    elif j == 1:
                        pe.wait_ge(q_read, at(b, c, 1, 1))
                    else:
                        pe.wait_ge(hid_ready, at(b, c, J, j - 1))
                    for n, w in enumerate((g_w, u_w)):
                        dst = ps[:, gate_bank(j) + n, :]
                        cols = slice(j * P, (j + 1) * P)
                        for k in range(KT):
                            nc.tensor.matmul(dst, w[0][:, k, cols], xh[:, c, k, :], start=(k == 0), stop=False)
                    with pe.If(wide_weights):
                        pe.wait_ge(ffn_lo, NF)
                        for n, w in enumerate((g_w, u_w)):
                            for k in range(KT):
                                nc.tensor.matmul(ps[:, gate_bank(j) + n, :], w[1][:, k, j * P:(j + 1) * P],
                                                 xh[:, c, k, :], start=False, stop=False)
                    for n, w in enumerate((g_w, u_w)):
                        for k in range(KT):
                            ins = nc.tensor.matmul(ps[:, gate_bank(j) + n, :], w[0][:, k, j * P:(j + 1) * P],
                                                   xl[:, c, k, :], start=False, stop=(k == KT - 1))
                    ins.then_inc(gu_done, 1)

                def down(p):
                    if p == 0:
                        if attend:
                            pe.wait_ge(out_ready, at(b - 1, c, 2, 2))
                        elif past:
                            pe.wait_ge(res_ready, at(b, c - 1, 2, 1))
                    elif ahead:
                        nb, ncx = (b, 1) if c == 0 else (b + 1, 0)
                        pe.wait_ge(xT_ready, at(nb, ncx, 2, 1))
                    else:
                        pe.wait_ge(y_ready, at(b - 1, c, 2, 2))
                    def both(h, w, j, start=False, stop=False):
                        for i in range(2):
                            t = slice((2 * p + i) * P, (2 * p + i + 1) * P)
                            ins = nc.tensor.matmul(ps[:, DOWN[p], i * D:(i + 1) * D], h[:, j, t], w[:, j, :],
                                                   start=start and i == 0, stop=stop, skip_group_check=True)
                        return ins

                    if zero and c == 0 and p == 0:
                        pe.wait_ge(ffn_hi, 3)
                    for j in range(J):
                        if p == 0:
                            pe.wait_ge(hh_ready, at(b, c, J, j + 1))
                        both(hh, d_w[0], j, start=(j == 0))
                    with pe.If(wide_weights):
                        for j in range(J):
                            both(hh, d_w[1], j)
                    for j in range(J):
                        if p == 0:
                            pe.wait_ge(hl_ready, at(b, c, J, j + 1))
                        ins = both(hl, d_w[0], j, stop=(j == J - 1))
                    ins.then_inc(down_done, 1)

                if feed:
                    project_kv(0)
                if attend:
                    query(0)
                    query(1)
                if feed:
                    project_kv(1)
                if attend:
                    query(2)
                    query(3)
                if feed:
                    project_q()
                if attend:
                    transpose_attn(0)
                    transpose_attn(1)
                if feed:
                    accumulate(0)
                    accumulate(1)
                if feed:
                    if zero and c == 0:
                        pe.wait_ge(ffn_hi, 2)
                        pe.wait_ge(wide_seen, 1)
                        flag[0] = pe.value_load(wide_any[0:1, 0:1].bitcast(I32))
                    wide_weights = flag[0]
                    gate_up(0)
                    gate_up(1)
                if attend:
                    project_y(0)
                if feed:
                    for j in range(2, J):
                        gate_up(j)
                if attend:
                    project_y(1)
                if ahead:
                    nb, ncx = (b, 1) if c == 0 else (b + 1, 0)
                    transpose_x(nb, ncx, attend, False)
                if feed:
                    down(0)
                    down(1)

            flag = [None]
            run(pe, step)


_T = ["L0_attn_Wq", "L0_attn_Wk", "L0_attn_Wv", "L0_attn_Wp", "L0_ffn_w_gate", "L0_ffn_w_up", "L0_ffn_w_down"]
_INS = ["L0_attn_x", "L0_attn_Wq", "L0_attn_Wk", "L0_attn_Wv", "L0_attn_Wp", "L0_attn_bp", "L0_attn_conv_w",
        "L0_attn_conv_b", "L0_ffn_w_gate", "L0_ffn_w_up", "L0_ffn_w_down"]


def kernel(**inputs):
    import numpy as _np
    import concourse.bacc as _bacc
    from concourse import mybir as _mybir
    from concourse.bass_utils import run_bass_kernel_spmd as _run

    nc = _bacc.Bacc("TRN2", target_bir_lowering=False, num_devices=1)
    arrays, args = {}, []
    for name in _INS:
        a = _np.asarray(inputs[name])
        a = _np.ascontiguousarray(a.T if name in _T else a)
        arrays[f"in_{name}_dram"] = a
        args.append(nc.dram_tensor(f"in_{name}_dram", a.shape, _mybir.dt.from_np(a.dtype), kind="ExternalInput").ap())
    x = arrays["in_L0_attn_x_dram"]
    out = nc.dram_tensor("out_0_dram", x.shape, _mybir.dt.from_np(x.dtype), kind="ExternalOutput").ap()
    build(nc, *args, out)
    r = _run(nc, [arrays], core_ids=[0])
    return r.results[0]["out_0_dram"]
```

```python
from contextlib import ExitStack

import concourse.bass as bass
from concourse import mybir

ALU = mybir.AluOpType
ACT = mybir.ActivationFunctionType
AX = mybir.AxisListType
F32 = mybir.dt.float32
F16 = mybir.dt.float16
I32 = mybir.dt.int32

P = 128
CHUNK = 512
TILES = CHUNK // P
PAIR = 2 * P
BANK = 512
HEADS = 16
EPS = 1e-5
FFN_SCALE = 1.0 / 127.0
EXPONENT = 0x7F800000
EXACT_INT = 2048.0

X_UP = 2.0 ** 10
W_UP = 2.0 ** 14
H_DOWN = 2.0 ** -20
TINY = 2.0 ** -96


def build(nc, x, wqT, wkT, wvT, wpT, bp, conv_w, conv_b, wgT, wuT, wdT, out):
    NB, S, D = x.shape
    HID = wgT.shape[1]
    KT = D // P
    J = HID // P
    HPB = HEADS // KT
    HD = D // HEADS
    CB = S // CHUNK
    AW = P + HPB
    VW = P + 1
    assert CB == 2 and KT == 2 and TILES == 4 and KT * D == BANK and KT * PAIR == BANK

    x_v = x.rearrange("b (c i p) d -> (b c) p i d", c=CB, p=P)
    out_v = out.rearrange("b (c i p) d -> (b c) p i d", c=CB, p=P)

    def at(b, c, per_step, k):
        return b * (CB * per_step) + (c * per_step + k)

    with ExitStack() as ctx:
        def sb(name, shape, dt=F32):
            return ctx.enter_context(nc.sbuf_tensor(name, shape, dt))

        def sem(name):
            return ctx.enter_context(nc.semaphore(name))

        names = ["q", "k", "v", "p"]
        w_raw = {n: sb(f"w{n}_raw", [P, KT, D]) for n in names}
        ffn_raw = {n: sb(f"w{n}_int", [P, HID * D // P], I32) for n in "gud"}
        kv_w = [sb(f"kv_w{h}", [P, KT, 2 * D], F16) for h in "hl"]
        q_w = [sb(f"q_w{h}", [P, KT, D], F16) for h in "hl"]
        p_w = [sb(f"p_w{h}", [P, KT, D], F16) for h in "hl"]
        g_w = [sb(f"g_w{h}", [P, KT, HID], F16) for h in "hl"]
        u_w = [sb(f"u_w{h}", [P, KT, HID], F16) for h in "hl"]
        d_w = [sb(f"d_w{h}", [P, J, D], F16) for h in "hl"]
        cw_raw = sb("cw_raw", [P, KT, 3])
        cb_raw = sb("cb_raw", [P, KT])
        cw = sb("cw", [P, KT, 3])
        cb = sb("cb", [P, KT])
        bp_sb = sb("bp_sb", [P, D])
        ident = sb("ident", [P, P])
        head_mask = sb("head_mask", [P, P])
        half = sb("half", [P, TILES])

        A_COLS = {"k": 0, "v": 1, "q": 2, "p": 3, "cw": 4, "cb": 5}
        F_COLS = {"g": 0, "u": 1, "d": 2}
        EARLY = 2
        NA, NF = len(A_COLS), len(F_COLS)
        a_max = sb("a_max", [P, NA]); a_all = sb("a_all", [P, NA])
        a_pow = sb("a_pow", [P, NA]); a_up = sb("a_up", [P, NA])
        f_max = sb("f_max", [P, NF]); f_all = sb("f_all", [P, NF])
        f_pow = sb("f_pow", [P, NF]); f_up = sb("f_up", [P, NF])
        y_sc = sb("y_sc", [P, 11])
        f_sc = sb("f_sc", [P, 6])
        wide = sb("wide", [P, NF]); wide_any = sb("wide_any", [P, 1])

        def a_col(of, name):
            return of[:, A_COLS[name]:A_COLS[name] + 1]

        q_down, k_down = y_sc[:, 0:1], y_sc[:, 1:2]
        y_up, tap_up, attn_to_y, y_down = y_sc[:, 2:3], y_sc[:, 3:4], y_sc[:, 4:5], y_sc[:, 5:6]
        silu_in, h_mul, f_down = f_sc[:, 0:1], f_sc[:, 1:2], f_sc[:, 2:3]
        q_flip, k_flip = y_sc[:, 9:10], y_sc[:, 10:11]

        x_in = sb("x_in", [P, CB, TILES, D])
        bn_raw = sb("bn_raw", [P, CB, TILES, 6])
        ln_tmp = sb("ln_tmp", [P, 5, TILES])
        neg_mean = sb("neg_mean", [P, CB, TILES])
        var_eps = sb("var_eps", [P, CB, TILES])
        rstd = sb("rstd", [P, CB, TILES])
        xn = sb("xn", [P, TILES, D])
        xb = sb("xb", [P, CB, TILES, D])
        xT = sb("xT", [P, CB, KT, CHUNK + 2])
        xh = sb("xh", [P, CB, KT, CHUNK], F16)
        xl = sb("xl", [P, CB, KT, CHUNK], F16)
        k_neg = sb("k_neg", [P, 2, 2, D])
        k_exp = sb("k_exp", [P, 2, 2, D])
        k_relu = sb("k_relu", [P, 2, 2, D])
        k_sb = sb("k_sb", [P, TILES, D])
        v_sb = sb("v_sb", [P, TILES, KT, VW])
        q_neg = sb("q_neg", [P, KT, CHUNK])
        q_exp = sb("q_exp", [P, KT, CHUNK])
        q_relu = sb("q_relu", [P, KT, CHUNK])
        q_sb = sb("q_sb", [P, CB, KT, CHUNK])
        state = sb("state", [P, KT, AW])
        den = sb("den", [P, TILES, KT, HPB])
        rden = sb("rden", [P, TILES, KT, HPB])
        attn = sb("attn", [P, TILES, D])
        local = sb("local", [P, KT, S])
        tap_part = sb("tap_part", [P, KT, CHUNK])
        y = sb("y", [P, KT, CHUNK])
        yh = sb("yh", [P, KT, CHUNK], F16)
        yl = sb("yl", [P, KT, CHUNK], F16)
        act_g = sb("act_g", [P, 2, CHUNK])
        hid = sb("hid", [P, 2, CHUNK])
        hh = sb("hh", [P, J, CHUNK], F16)
        hl = sb("hl", [P, J, CHUNK], F16)
        res = sb("res", [P, CB, TILES, D])
        out_sb = sb("out_sb", [P, CB, TILES, D])

        ps = ctx.enter_context(nc.psum_tensor("ps", [P, 8, BANK], F32))
        def gate_bank(j):
            return 2 * ((j + 1) % 2)
        RING = [4, 5, 7]
        STATE = 6
        QKV = [RING[i % 3] for i in range(4)]
        YT = [RING[4 % 3], RING[5 % 3]]
        WP = [RING[6 % 3], RING[7 % 3]]
        XT = [RING[8 % 3], RING[9 % 3]]
        DOWN = [RING[10 % 3], RING[11 % 3]]
        LAST_QKV = [[7, STATE, 4, 5], [2, 3, 0, 1]]
        LAST_YT = [[7, STATE], [2, 0]]
        LAST_WP = [[7, STATE], [3, 1]]
        LAST_DOWN = [4, 5]

        def halves(bank):
            return ps[:, bank, :].rearrange("p (k n) -> p k n", k=2)

        w_in = {n: sem(f"w{n}_loaded") for n in ["q", "k", "v", "p", "g", "u", "d"]}
        small_in = sem("small_loaded")
        consts = sem("consts_made")
        ones_made = sem("ones_made")
        kv_maxed, kv_reduced, kv_scaled = sem("kv_maxed"), sem("kv_reduced"), sem("kv_scaled")
        a_maxed, a_reduced, a_scaled = sem("a_maxed"), sem("a_reduced"), sem("a_scaled")
        f_maxed, f_reduced, f_scaled = sem("f_maxed"), sem("f_reduced"), sem("f_scaled")
        small_op = sem("scale_steps")
        kv_hi, kv_lo, qp_hi, qp_lo = sem("kv_hi"), sem("kv_lo"), sem("qp_hi"), sem("qp_lo")
        ffn_hi, ffn_lo = sem("ffn_hi"), sem("ffn_lo")
        wide_seen = sem("wide_seen")
        taps_made = sem("taps_made")
        x_loaded = [sem(f"x_loaded{c}") for c in range(CB)]
        out_stored = [sem(f"out_stored{c}") for c in range(CB)]
        bn_seen, bn_merged, ln_ready = sem("bn_seen"), sem("bn_merged"), sem("ln_ready")
        bn_squared, bn_var = sem("bn_squared"), sem("bn_var")
        rstd_ready, xn_ready, xb_ready = sem("rstd_ready"), sem("xn_ready"), sem("xb_ready")
        xT_done, xT_ready, xl_ready = sem("xT_done"), sem("xT_ready"), sem("xl_ready")
        kv_done, k_parts, v_ready, k_ready = sem("kv_done"), sem("k_parts"), sem("v_ready"), sem("k_ready")
        acc_done, state_ready = sem("acc_done"), sem("state_ready")
        q_done, q_parts, q_ready = sem("q_done"), sem("q_parts"), sem("q_ready")
        k_flipped, q_flipped, q_read = sem("k_flipped"), sem("q_flipped"), sem("q_read")
        qkv_done, den_kept, den_inv, attn_ready = sem("qkv_done"), sem("den_kept"), sem("den_inv"), sem("attn_ready")
        yT_done, y_ready, yh_ready, yl_ready = sem("yT_done"), sem("y_ready"), sem("yh_ready"), sem("yl_ready")
        wp_done, out_ready = sem("wp_done"), sem("out_ready")
        gu_done, silu_ready, hid_ready = sem("gu_done"), sem("silu_ready"), sem("hid_ready")
        hh_ready, hl_ready, down_done, res_ready = sem("hh_ready"), sem("hl_ready"), sem("down_done"), sem("res_ready")
        tap_scaled = sem("tap_scaled")
        mid_tap, left_tap, conv_done = sem("mid_tap"), sem("left_tap"), sem("conv_done")

        block = ctx.enter_context(nc.Block())

        def run(eng, step):
            step(0, 0, False, True)
            step(0, 1, False, True)
            with eng.Fori(1, NB - 1) as b:
                step(b, 0, True, True)
                step(b, 1, True, True)
            step(NB - 1, 0, True, True)
            step(NB - 1, 1, True, False)

        @block.sync
        def _(sp):
            sp.dma_start(x_in[:, 0, :, :], x_v[0]).then_inc(x_loaded[0], 16)
            sp.dma_start(cw_raw[:, :, :], conv_w.rearrange("(k p) t -> p k t", p=P)).then_inc(small_in, 16)
            sp.dma_start(cb_raw[:, :], conv_b.rearrange("(k p) -> p k", p=P),
                         allow_slow_non_contiguous=True).then_inc(small_in, 16)
            for n, w in (("q", wqT), ("p", wpT)):
                sp.dma_start(w_raw[n][:, :, :], w.rearrange("(k p) n -> p k n", p=P)).then_inc(w_in[n], 16)
            sp.dma_start(bp_sb[:, :], bp.rearrange("(o n) -> o n", o=1).broadcast_to([P, D])).then_inc(small_in, 16)
            for n, w in (("g", wgT), ("u", wuT), ("d", wdT)):
                sp.dma_start(ffn_raw[n][:, :].rearrange("p (k n) -> p k n", n=w.shape[1]),
                             w.rearrange("(k p) n -> p k n", p=P)).then_inc(w_in[n], 16)
                if n == "g":
                    sp.dma_start(x_in[:, 1, :, :], x_v[1]).then_inc(x_loaded[1], 16)

            def store(b, c):
                sp.wait_ge(out_ready, at(b, c, 2, 2))
                sp.dma_start(out_v[b * CB + c], out_sb[:, c, :, :]).then_inc(out_stored[c], 16)

            def step(b, c, attend, ahead):
                if attend:
                    store(b - 1, c)
                if not (isinstance(b, int) and b == NB - 1):
                    if isinstance(b, int) and b == 0 and c == 0:
                        sp.wait_ge(xb_ready, 1)
                    sp.wait_ge(xn_ready, at(b, c, 2, 2))
                    sp.dma_start(x_in[:, c, :, :], x_v[CB * b + (c + CB)]).then_inc(x_loaded[c], 16)

            run(sp, step)
            for c in range(CB):
                store(NB - 1, c)
            for c in range(CB):
                sp.wait_ge(out_stored[c], 16 * NB)

        @block.gpsimd
        def _(pool):
            def add_bias(b, c):
                nc.gpsimd.tensor_tensor(xb[:, c, :, :], x_in[:, c, :, :],
                                        bp_sb[:, :].unsqueeze(1).broadcast_to([P, TILES, D]),
                                        ALU.add).then_inc(xb_ready, 1)

            def normalise(c, i):
                return nc.gpsimd.tensor_scalar(xn[:, i, :], x_in[:, c, i, :], neg_mean[:, c, i:i + 1],
                                               rstd[:, c, i:i + 1], ALU.add, ALU.mult)

            def layernorm(b, c):
                pool.wait_ge(ln_ready, at(b, c, 1, 1))
                nc.gpsimd.tensor_tensor(rstd[:, c, :], var_eps[:, c, :], half[:, :], ALU.pow).then_inc(rstd_ready, 1)
                pool.wait_ge(rstd_ready, at(b, c, 1, 1))
                pool.wait_ge(xT_done, at(b, c - 1, 2, 2))
                add_bias(b, c)
                for i in range(TILES):
                    ins = normalise(c, i)
                    if i % 2 == 1:
                        ins.then_inc(xn_ready, 1)

            def across(dst, src):
                return nc.gpsimd.partition_all_reduce(dst, src, P, bass.bass_isa.ReduceOp.max)

            nc.gpsimd.memset(half[:, :], -0.5).then_inc(consts, 1)
            nc.gpsimd.memset(ident[:, :], 0.0).then_inc(consts, 1)
            nc.gpsimd.memset(head_mask[:, :], 1.0).then_inc(consts, 1)
            nc.gpsimd.memset(v_sb[:, :, :, P:VW], 1.0).then_inc(ones_made, 1)
            nc.gpsimd.memset(xT[:, 0, :, 0:1], 0.0).then_inc(ones_made, 1)
            nc.gpsimd.memset(xT[:, 1, :, CHUNK + 1:CHUNK + 2], 0.0).then_inc(ones_made, 1)
            pool.wait_ge(consts, 3)
            nc.gpsimd.affine_select(out=ident[:, :], in_=ident[:, :], compare_op=ALU.not_equal, fill=1.0,
                                    base=0, pattern=[[-1, P]], channel_multiplier=1).then_inc(consts, 1)
            hm = head_mask[:, :].rearrange("p (h e) -> p h e", h=HPB)
            nc.gpsimd.affine_select(out=hm, in_=hm, compare_op=ALU.is_ge, fill=0.0, base=0,
                                    pattern=[[-HD, HPB], [0, HD]], channel_multiplier=1).then_inc(consts, 1)
            pool.wait_ge(consts, 5)
            nc.gpsimd.affine_select(out=hm, in_=hm, compare_op=ALU.is_ge, fill=0.0, base=HD - 1,
                                    pattern=[[HD, HPB], [0, HD]], channel_multiplier=-1).then_inc(consts, 1)
            pool.wait_ge(ln_ready, 1)
            nc.gpsimd.tensor_tensor(rstd[:, 0, :], var_eps[:, 0, :], half[:, :], ALU.pow).then_inc(rstd_ready, 1)
            pool.wait_ge(rstd_ready, 1)
            normalise(0, 0)
            normalise(0, 1).then_inc(xn_ready, 1)
            pool.wait_ge(kv_maxed, EARLY)
            across(a_all[:, 0:EARLY], a_max[:, 0:EARLY]).then_inc(kv_reduced, 1)
            normalise(0, 2)
            normalise(0, 3).then_inc(xn_ready, 1)
            pool.wait_ge(a_maxed, NA - EARLY)
            across(a_all[:, EARLY:NA], a_max[:, EARLY:NA]).then_inc(a_reduced, 1)
            pool.wait_ge(small_in, 48)
            add_bias(0, 0)
            pool.wait_ge(f_maxed, NF)
            across(f_all[:, :], f_max[:, :]).then_inc(f_reduced, 1)

            def step(b, c, attend, ahead):
                if ahead:
                    layernorm(*((b, 1) if c == 0 else (b + 1, 0)))

            run(pool, step)
            for side, done, before in ((0, left_tap, mid_tap), (2, conv_done, left_tap)):
                for k in range(KT):
                    pool.wait_ge(before, at(NB - 1, 1, KT, k + 1))
                    nc.gpsimd.tensor_scalar(tap_part[:, k, :], xT[:, 1, k, side:side + CHUNK],
                                            cw[:, k, side:side + 1], None, ALU.mult).then_inc(tap_scaled, 1)
                    pool.wait_ge(tap_scaled, side // 2 * KT + k + 1)
                    here = local[:, k, CHUNK:S]
                    nc.gpsimd.tensor_tensor(here, here, tap_part[:, k, :], ALU.add).then_inc(done, 1)

        @block.scalar
        def _(act):
            def transposed(b, c, first):
                for p in range(2):
                    act.wait_ge(xT_done, at(b, c, 2, p + 1))
                    src = halves(XT[p])
                    if p == 0 and not (isinstance(b, int) and b == 0):
                        act.wait_ge(conv_done, at(b, c, KT, -KT))
                    nc.scalar.activation(xT[:, c, :, 1 + p * PAIR:1 + (p + 1) * PAIR], src, ACT.Copy)
                    if c == 1 and p == 0:
                        nc.scalar.activation(xT[:, 0, :, CHUNK + 1:CHUNK + 2], src[:, :, 0:1], ACT.Copy)
                        act.wait_ge(xT_ready, at(b, 0, 2, 2))
                        nc.scalar.activation(xT[:, 1, :, 0:1], xT[:, 0, :, CHUNK:CHUNK + 1], ACT.Copy)
                    nc.scalar.activation(xh[:, c, :, p * PAIR:(p + 1) * PAIR], src, ACT.Copy).then_inc(xT_ready, 1)

            for n, w in (("k", wkT), ("v", wvT)):
                act.dma_start(w_raw[n][:, :, :], w.rearrange("(k p) n -> p k n", p=P)).then_inc(w_in[n], 16)
            nc.scalar.preload_act_table(ACT.Exp)

            def high(dst, src, scale, done):
                nc.scalar.activation(dst, src, ACT.Copy, scale=scale).then_inc(done, 1)

            act.wait_ge(kv_scaled, 1)
            high(kv_w[0][:, :, 0:D], w_raw["k"][:, :, :], a_col(a_up, "k"), kv_hi)
            high(kv_w[0][:, :, D:2 * D], w_raw["v"][:, :, :], a_col(a_up, "v"), kv_hi)
            transposed(0, 0, True)
            act.wait_ge(a_scaled, 1)
            high(q_w[0][:, :, :], w_raw["q"][:, :, :], a_col(a_up, "q"), qp_hi)
            high(p_w[0][:, :, :], w_raw["p"][:, :, :], a_col(a_up, "p"), qp_hi)

            def middle_tap(b, c, k):
                if k == 0:
                    if not (isinstance(b, int) and b == 0):
                        act.wait_ge(y_ready, at(b - 1, c, 2, 2))
                    elif c == 0:
                        act.wait_ge(taps_made, 2)
                nc.scalar.activation(local[:, k, c * CHUNK:(c + 1) * CHUNK], xT[:, c, k, 1:1 + CHUNK],
                                     ACT.Identity, scale=cw[:, k, 1:2], bias=cb[:, k:k + 1]).then_inc(mid_tap, 1)

            def y_high(b, c, p):
                cols = slice(p * PAIR, (p + 1) * PAIR)
                act.wait_ge(y_ready, at(b, c, 2, p + 1))
                nc.scalar.activation(yh[:, :, cols], y[:, :, cols], ACT.Copy).then_inc(yh_ready, 1)

            def step(b, c, attend, ahead):
                past = not (isinstance(b, int) and b == 0 and c == 0)

                def key_parts(p):
                    bank = 2 * p
                    act.wait_ge(kv_done, at(b, c, 2, p + 1))
                    if past:
                        act.wait_ge(k_ready, at(b, c - 1, 2, p + 1))
                    nc.scalar.activation(k_neg[:, p, :, :], ps[:, bank:bank + 2, 0:D], ACT.Relu,
                                         scale=k_flip).then_inc(k_flipped, 1)
                    nc.scalar.activation(k_relu[:, p, :, :], ps[:, bank:bank + 2, 0:D], ACT.Relu,
                                         scale=k_down)
                    if past:
                        act.wait_ge(acc_done, at(b, c - 1, 2, p + 1))
                    elif p == 0:
                        act.wait_ge(ones_made, 3)
                    for i in range(2):
                        ins = nc.scalar.activation(v_sb[:, 2 * p + i, :, 0:P],
                                                   ps[:, bank + i, D:2 * D].rearrange("p (k n) -> p k n", k=KT),
                                                   ACT.Copy)
                    ins.then_inc(v_ready, 1)
                    act.wait_ge(k_flipped, at(b, c, 2, p + 1))
                    nc.scalar.activation(k_exp[:, p, :, :], k_neg[:, p, :, :], ACT.Exp,
                                         scale=-1.0).then_inc(k_parts, 1)

                def query_parts():
                    act.wait_ge(q_done, at(b, c, 1, 1))
                    if past:
                        act.wait_ge(q_ready, at(b, c - 1, 1, 1))
                    nc.scalar.activation(q_neg[:, :, :], ps[:, 0:2, :], ACT.Relu, scale=q_flip).then_inc(q_flipped, 1)
                    nc.scalar.activation(q_relu[:, :, :], ps[:, 0:2, :], ACT.Relu, scale=q_down).then_inc(q_read, 1)
                    act.wait_ge(q_flipped, at(b, c, 1, 1))
                    nc.scalar.activation(q_exp[:, :, :], q_neg[:, :, :], ACT.Exp, scale=-1.0).then_inc(q_parts, 1)

                def silu(j):
                    act.wait_ge(gu_done, at(b, c, J, j + 1))
                    if past or j >= 2:
                        act.wait_ge(hid_ready, at(b, c, J, j - 1))
                    nc.scalar.activation(act_g[:, j % 2, :], ps[:, gate_bank(j), :], ACT.Silu,
                                         scale=silu_in).then_inc(silu_ready, 1)

                def hidden_high(j):
                    act.wait_ge(hid_ready, at(b, c, J, j + 1))
                    if past and j == 0:
                        act.wait_ge(down_done, at(b, c - 1, 2, 2))
                    nc.scalar.activation(hh[:, j, :], hid[:, j % 2, :], ACT.Copy).then_inc(hh_ready, 1)

                if past:
                    act.wait_ge(xT_ready, at(b, c, 2, 1))
                    for k in range(KT):
                        middle_tap(*((b, 0) if c == 1 else (b - 1, 1)), k)
                key_parts(0)
                key_parts(1)
                query_parts()
                if attend:
                    y_high(b - 1, c, 0)
                    y_high(b - 1, c, 1)
                if not past:
                    act.wait_ge(f_scaled, 1)
                    high(d_w[0][:, :, :], ffn_raw["d"][:, :].rearrange("p (k n) -> p k n", k=J), f_up[:, 2:3], ffn_hi)
                nc.scalar.preload_act_table(ACT.Silu)
                for j in range(J):
                    silu(j)
                    if j >= 1:
                        hidden_high(j - 1)
                    if not ahead and j in (1, 2):
                        middle_tap(b, c, j - 1)
                hidden_high(J - 1)
                if ahead:
                    nc.scalar.preload_act_table(ACT.Exp)
                    transposed(*((b, 1) if c == 0 else (b + 1, 0)), False)
                else:
                    for ac in range(CB):
                        y_high(b, ac, 0)
                        y_high(b, ac, 1)

            run(act, step)

        @block.vector
        def _(dve):
            def stats(b, c):
                dve.wait_ge(x_loaded[c], (b + 1) * 16)
                for i in range(TILES):
                    nc.vector.bn_stats(bn_raw[:, c, i, :], x_in[:, c, i, :]).then_inc(bn_seen, 1)
                even, odd = bn_raw[:, c, :, 0:3], bn_raw[:, c, :, 3:6]
                total, apart, spread, square, var = (ln_tmp[:, n, :] for n in range(5))
                dve.wait_ge(bn_seen, at(b, c, TILES, TILES))
                nc.vector.tensor_tensor(apart, even[:, :, 1], odd[:, :, 1], ALU.subtract)
                nc.vector.tensor_tensor(spread, even[:, :, 2], odd[:, :, 2], ALU.add)
                nc.vector.tensor_tensor(total, even[:, :, 1], odd[:, :, 1], ALU.add).then_inc(bn_merged, 1)
                dve.wait_ge(bn_merged, at(b, c, 1, 1))
                nc.vector.tensor_scalar(neg_mean[:, c, :], total, -0.5, None, ALU.mult)
                nc.vector.scalar_tensor_tensor(out=square, in0=apart, scalar=0.25, in1=apart, op0=ALU.mult,
                                               op1=ALU.mult).then_inc(bn_squared, 1)
                dve.wait_ge(bn_squared, at(b, c, 1, 1))
                nc.vector.scalar_tensor_tensor(out=var, in0=spread, scalar=1.0 / D, in1=square, op0=ALU.mult,
                                               op1=ALU.add).then_inc(bn_var, 1)
                dve.wait_ge(bn_var, at(b, c, 1, 1))
                nc.vector.tensor_scalar(var_eps[:, c, :], var, EPS, X_UP ** -2,
                                        ALU.add, ALU.mult).then_inc(ln_ready, 1)

            def x_low(b, c):
                for p in range(2):
                    cols = slice(p * PAIR, (p + 1) * PAIR)
                    dve.wait_ge(xT_ready, at(b, c, 2, p + 1))
                    nc.vector.tensor_tensor(xl[:, c, :, cols], xT[:, c, :, 1 + p * PAIR:1 + (p + 1) * PAIR], xh[:, c, :, cols],
                                            ALU.subtract).then_inc(xl_ready, 1)

            ops = [0]

            def scale_op(ins):
                ops[0] += 1
                ins.then_inc(small_op, 1)
                dve.wait_ge(small_op, ops[0])

            def powers(pow_, up, largest):
                scale_op(nc.vector.tensor_scalar(pow_, largest, TINY, None, ALU.max))
                scale_op(nc.vector.tensor_scalar(pow_.bitcast(I32), pow_.bitcast(I32), EXPONENT, None,
                                                 ALU.bitwise_and))
                scale_op(nc.vector.reciprocal(up, pow_))
                scale_op(nc.vector.tensor_scalar(up, up, W_UP, None, ALU.mult))

            def largest(dst, src, dims):
                return nc.vector.tensor_reduce(dst, src, dims, ALU.max, apply_absolute_value=True)

            def low(dst, src, scale, hi, halved, n, done):
                dve.wait_ge(halved, n)
                nc.vector.scalar_tensor_tensor(out=dst, in0=src, scalar=scale, in1=hi, op0=ALU.mult,
                                               op1=ALU.subtract).then_inc(done, 1)

            def attention_maxima(names, done):
                for n in names:
                    dve.wait_ge(w_in[n], 16)
                    largest(a_col(a_max, n), w_raw[n][:, :, :], AX.XY).then_inc(done, 1)

            def ffn_maximum(n):
                dve.wait_ge(w_in[n], 16)
                largest(f_max[:, F_COLS[n]:F_COLS[n] + 1], ffn_raw[n][:, :], AX.X).then_inc(f_maxed, 1)

            stats(0, 0)
            attention_maxima(["k", "v"], kv_maxed)
            attention_maxima(["q", "p"], a_maxed)
            dve.wait_ge(small_in, 48)
            largest(a_col(a_max, "cw"), cw_raw[:, :, :], AX.XY).then_inc(a_maxed, 1)
            largest(a_col(a_max, "cb"), cb_raw[:, :], AX.X).then_inc(a_maxed, 1)
            dve.wait_ge(kv_reduced, 1)
            powers(a_pow[:, 0:EARLY], a_up[:, 0:EARLY], a_all[:, 0:EARLY])
            nc.vector.tensor_scalar(k_flip, a_col(a_pow, "k"), -1.0 / (X_UP * W_UP), None, ALU.mult)
            nc.vector.tensor_scalar(k_down, a_col(a_pow, "k"), 1.0 / (X_UP * W_UP), None,
                                    ALU.mult).then_inc(kv_scaled, 1)
            low(kv_w[1][:, :, 0:D], w_raw["k"][:, :, :], a_col(a_up, "k"), kv_w[0][:, :, 0:D], kv_hi, 1, kv_lo)
            low(kv_w[1][:, :, D:2 * D], w_raw["v"][:, :, :], a_col(a_up, "v"), kv_w[0][:, :, D:2 * D], kv_hi, 2, kv_lo)
            x_low(0, 0)
            dve.wait_ge(a_reduced, 1)
            powers(a_pow[:, EARLY:NA], a_up[:, EARLY:NA], a_all[:, EARLY:NA])
            nc.vector.tensor_scalar(q_flip, a_col(a_pow, "q"), -1.0 / (X_UP * W_UP), None, ALU.mult)
            nc.vector.tensor_scalar(q_down, a_col(a_pow, "q"), 1.0 / (X_UP * W_UP), None, ALU.mult).then_inc(a_scaled, 1)
            ffn_maximum("g")
            low(q_w[1][:, :, :], w_raw["q"][:, :, :], a_col(a_up, "q"), q_w[0][:, :, :], qp_hi, 1, qp_lo)
            low(p_w[1][:, :, :], w_raw["p"][:, :, :], a_col(a_up, "p"), p_w[0][:, :, :], qp_hi, 2, qp_lo)
            ffn_maximum("u")
            ffn_maximum("d")

            def ffn_scales():
                dve.wait_ge(f_reduced, 1)
                powers(f_pow[:, :], f_up[:, :], f_all[:, :])
                nc.vector.tensor_scalar(silu_in, f_pow[:, 0:1], FFN_SCALE / (X_UP * W_UP), None, ALU.mult)
                nc.vector.tensor_scalar(h_mul, f_up[:, 0:1], H_DOWN / W_UP, None, ALU.mult)
                nc.vector.tensor_scalar(wide[:, :], f_all[:, :], EXACT_INT, None, ALU.is_gt)
                scale_op(nc.vector.scalar_tensor_tensor(out=f_sc[:, 3:4], in0=f_pow[:, 0:1],
                                                        scalar=FFN_SCALE ** 2 / (H_DOWN * X_UP * W_UP * W_UP),
                                                        in1=f_pow[:, 1:2], op0=ALU.mult, op1=ALU.mult))
                nc.vector.tensor_reduce(wide_any[:, :], wide[:, :], AX.X, ALU.max).then_inc(wide_seen, 1)
                nc.vector.tensor_tensor(f_down, f_sc[:, 3:4], f_pow[:, 2:3], ALU.mult).then_inc(f_scaled, 1)

            def ffn_high(n, w):
                i = F_COLS[n]
                nc.vector.tensor_scalar(w[0][:, :, :], ffn_raw[n][:, :].rearrange("p (k n) -> p k n", k=KT),
                                        f_up[:, i:i + 1], None, ALU.mult).then_inc(ffn_hi, 1)

            def ffn_low_halves():
                dve.wait_ge(wide_seen, 1)
                any_wide = dve.value_load(wide_any[0:1, 0:1].bitcast(I32))
                with dve.If(any_wide):
                    for i, (n, w, k) in enumerate((("g", g_w, KT), ("u", u_w, KT), ("d", d_w, J))):
                        low(w[1][:, :, :], ffn_raw[n][:, :].rearrange("p (k n) -> p k n", k=k), f_up[:, i:i + 1],
                            w[0][:, :, :], ffn_hi, NF, ffn_lo)

            def attention_scales():
                t = [y_sc[:, 6:7], y_sc[:, 7:8], y_sc[:, 8:9]]
                scale_op(nc.vector.tensor_scalar(t[0], a_col(a_pow, "v"), 512.0, None, ALU.mult))
                scale_op(nc.vector.scalar_tensor_tensor(out=t[1], in0=a_col(a_pow, "cw"), scalar=128.0, in1=t[0],
                                                        op0=ALU.mult, op1=ALU.add))
                scale_op(nc.vector.scalar_tensor_tensor(out=t[0], in0=a_col(a_pow, "cb"), scalar=2.0, in1=t[1],
                                                        op0=ALU.mult, op1=ALU.add))
                scale_op(nc.vector.tensor_scalar(t[1].bitcast(I32), t[0].bitcast(I32), EXPONENT, None,
                                                 ALU.bitwise_and))
                scale_op(nc.vector.reciprocal(t[2], t[1]))
                scale_op(nc.vector.tensor_scalar(y_up, t[2], W_UP, None, ALU.mult))
                nc.vector.tensor_scalar(cb[:, :], cb_raw[:, :], y_up, None, ALU.mult).then_inc(taps_made, 1)
                nc.vector.scalar_tensor_tensor(out=attn_to_y, in0=a_col(a_pow, "v"), scalar=1.0 / (X_UP * W_UP),
                                               in1=y_up, op0=ALU.mult, op1=ALU.mult)
                nc.vector.scalar_tensor_tensor(out=y_down, in0=a_col(a_pow, "p"), scalar=W_UP ** -2, in1=t[1],
                                               op0=ALU.mult, op1=ALU.mult)
                scale_op(nc.vector.tensor_scalar(tap_up, y_up, 1.0 / X_UP, None, ALU.mult))
                nc.vector.tensor_scalar(cw[:, :, :], cw_raw[:, :, :], tap_up, None, ALU.mult).then_inc(taps_made, 1)

            def normalise(b, c, p, banks):
                tiles = (2 * p, 2 * p + 1)
                src = {i: ps[:, banks[i], 0:KT * AW].rearrange("p (k n) -> p k n", k=KT) for i in tiles}
                for i in tiles:
                    dve.wait_ge(qkv_done, at(b, c, TILES, i + 1))
                    nc.vector.tensor_scalar(den[:, i, :, :], src[i][:, :, P:AW], 1e-6, None,
                                            ALU.max).then_inc(den_kept, 1)
                for i in tiles:
                    dve.wait_ge(den_kept, at(b, c, TILES, i + 1))
                    nc.vector.reciprocal(rden[:, i, :, :], den[:, i, :, :]).then_inc(den_inv, 1)
                for i in tiles:
                    dve.wait_ge(den_inv, at(b, c, TILES, i + 1))
                    nc.vector.tensor_tensor(attn[:, i, :].rearrange("p (k h e) -> p k h e", k=KT, h=HPB),
                                            src[i][:, :, 0:P].rearrange("p k (h e) -> p k h e", h=HPB),
                                            rden[:, i, :, :].unsqueeze(3).broadcast_to([P, KT, HPB, HD]),
                                            ALU.mult).then_inc(attn_ready, 1)

            def put_y(b, c, p, banks):
                cols = slice(p * PAIR, (p + 1) * PAIR)
                dve.wait_ge(yT_done, at(b, c, 2, p + 1))
                if p == 0:
                    dve.wait_ge(conv_done, at(b, c, KT, KT))
                if not (isinstance(b, int) and b == 0 and c == 0):
                    dve.wait_ge(yl_ready, at(b, c, 2, p - 1))
                    dve.wait_ge(wp_done, at(b, c, 2, p - 1))
                nc.vector.scalar_tensor_tensor(out=y[:, :, cols], in0=halves(banks[p]), scalar=attn_to_y,
                                               in1=local[:, :, c * CHUNK + p * PAIR:c * CHUNK + (p + 1) * PAIR],
                                               op0=ALU.mult, op1=ALU.add).then_inc(y_ready, 1)

            def y_low(b, c, p):
                cols = slice(p * PAIR, (p + 1) * PAIR)
                dve.wait_ge(yh_ready, at(b, c, 2, p + 1))
                nc.vector.tensor_tensor(yl[:, :, cols], y[:, :, cols], yh[:, :, cols],
                                        ALU.subtract).then_inc(yl_ready, 1)

            def output(b, c, p, banks):
                dve.wait_ge(wp_done, at(b, c, 2, p + 1))
                dve.wait_ge(res_ready, at(b, c, 2, p + 1))
                if not (isinstance(b, int) and b == 0):
                    dve.wait_ge(out_stored[c], b * 16)
                nc.vector.scalar_tensor_tensor(out=out_sb[:, c, 2 * p:2 * p + 2, :], in0=halves(banks[p]),
                                               scalar=y_down, in1=res[:, c, 2 * p:2 * p + 2, :],
                                               op0=ALU.mult, op1=ALU.add).then_inc(out_ready, 1)

            def tap(b, c, k, side):
                done, before = (left_tap, mid_tap) if side == 0 else (conv_done, left_tap)
                dve.wait_ge(before, at(b, c, KT, k + 1))
                here = local[:, k, c * CHUNK:(c + 1) * CHUNK]
                nc.vector.scalar_tensor_tensor(out=here, in0=xT[:, c, k, side:side + CHUNK],
                                               scalar=cw[:, k, side:side + 1], in1=here,
                                               op0=ALU.mult, op1=ALU.add).then_inc(done, 1)

            def step(b, c, attend, ahead):
                past = not (isinstance(b, int) and b == 0 and c == 0)
                nb, ncx = (b, 1) if c == 0 else (b + 1, 0)
                if past:
                    pb, pc = (b, 0) if c == 1 else (b - 1, 1)

                def put_k(p):
                    dve.wait_ge(k_parts, at(b, c, 2, p + 1))
                    if past:
                        dve.wait_ge(acc_done, at(b, c - 1, 2, p + 1))
                    nc.vector.tensor_tensor(k_sb[:, 2 * p:2 * p + 2, :], k_exp[:, p, :, :], k_relu[:, p, :, :],
                                            ALU.add).then_inc(k_ready, 1)

                def put_q():
                    dve.wait_ge(q_parts, at(b, c, 1, 1))
                    nc.vector.tensor_tensor(q_sb[:, c, :, :], q_exp[:, :, :], q_relu[:, :, :],
                                            ALU.add).then_inc(q_ready, 1)

                def put_state():
                    dve.wait_ge(acc_done, at(b, c, 2, 2))
                    acc = halves(STATE)
                    for k in range(KT):
                        nc.vector.tensor_tensor(state[:, k, 0:P], acc[:, k, 0:P], head_mask[:, :], ALU.mult)
                        ins = nc.vector.tensor_scalar(state[:, k, P:AW], head_mask[:, 0:P:HD],
                                                      acc[:, k, P:P + 1], None, ALU.mult)
                    ins.then_inc(state_ready, 1)

                def hidden(j):
                    dve.wait_ge(silu_ready, at(b, c, J, j + 1))
                    if past or j >= 2:
                        dve.wait_ge(hl_ready, at(b, c, J, j - 1))
                    nc.vector.scalar_tensor_tensor(out=hid[:, j % 2, :], in0=act_g[:, j % 2, :], scalar=h_mul,
                                                   in1=ps[:, gate_bank(j) + 1, :], op0=ALU.mult,
                                                   op1=ALU.mult).then_inc(hid_ready, 1)

                def hidden_low(j):
                    dve.wait_ge(hh_ready, at(b, c, J, j + 1))
                    nc.vector.tensor_tensor(hl[:, j, :], hid[:, j % 2, :], hh[:, j, :],
                                            ALU.subtract).then_inc(hl_ready, 1)

                def put_res(p, banks):
                    dve.wait_ge(down_done, at(b, c, 2, p + 1))
                    dve.wait_ge(xb_ready, at(b, c, 1, 1))
                    nc.vector.scalar_tensor_tensor(out=res[:, c, 2 * p:2 * p + 2, :], in0=halves(banks[p]),
                                                   scalar=f_down, in1=xb[:, c, 2 * p:2 * p + 2, :],
                                                   op0=ALU.mult, op1=ALU.add).then_inc(res_ready, 1)

                if past:
                    tap(pb, pc, 0, 0)
                    tap(pb, pc, 1, 0)
                if attend:
                    if ahead:
                        stats(nb, ncx)
                    normalise(b - 1, c, 0, QKV)
                if not past:
                    ffn_scales()
                    ffn_high("g", g_w)
                put_k(0)
                if not past:
                    ffn_high("u", u_w)
                else:
                    tap(pb, pc, 0, 2)
                if attend:
                    normalise(b - 1, c, 1, QKV)
                if past:
                    tap(pb, pc, 1, 2)
                put_k(1)
                if attend:
                    put_y(b - 1, c, 0, YT)
                    put_y(b - 1, c, 1, YT)
                    y_low(b - 1, c, 0)
                    y_low(b - 1, c, 1)
                else:
                    stats(nb, ncx)
                put_q()
                if not past:
                    ffn_low_halves()
                    attention_scales()
                if ahead:
                    for j in range(J):
                        hidden(j)
                        if j == J - 1 and attend:
                            output(b - 1, c, 1, WP)
                        if j >= 1:
                            hidden_low(j - 1)
                        if j == 1 and c == CB - 1:
                            put_state()
                        if j == 3 and attend:
                            output(b - 1, c, 0, WP)
                    hidden_low(J - 1)
                    x_low(nb, ncx)
                    put_res(0, DOWN)
                    put_res(1, DOWN)
                else:
                    hidden(0)
                    hidden(1)
                    hidden_low(0)
                    put_state()
                    hidden(2)
                    hidden_low(1)
                    output(b - 1, c, 0, WP)
                    hidden(3)
                    hidden_low(2)
                    output(b - 1, c, 1, WP)
                    normalise(b, 0, 0, LAST_QKV[0])
                    hidden(4)
                    hidden_low(3)
                    normalise(b, 0, 1, LAST_QKV[0])
                    hidden(5)
                    hidden_low(4)
                    put_y(b, 0, 0, LAST_YT[0])
                    put_y(b, 0, 1, LAST_YT[0])
                    hidden_low(5)
                    y_low(b, 0, 0)
                    y_low(b, 0, 1)
                    normalise(b, 1, 0, LAST_QKV[1])
                    normalise(b, 1, 1, LAST_QKV[1])
                    put_res(0, LAST_DOWN)
                    put_y(b, 1, 0, LAST_YT[1])
                    put_y(b, 1, 1, LAST_YT[1])
                    output(b, 0, 0, LAST_WP[0])
                    output(b, 0, 1, LAST_WP[0])
                    y_low(b, 1, 0)
                    y_low(b, 1, 1)
                    put_res(1, LAST_DOWN)
                    output(b, 1, 0, LAST_WP[1])
                    output(b, 1, 1, LAST_WP[1])

            step(0, 0, False, True)
            step(0, 1, False, True)
            step(1, 0, True, True)
            step(1, 1, True, True)
            with dve.Fori(2, NB - 1) as b:
                step(b, 0, True, True)
                step(b, 1, True, True)
            step(NB - 1, 0, True, True)
            step(NB - 1, 1, True, False)

        @block.tensor
        def _(pe):
            def transpose_x(b, c, attend, first):
                for p in range(2):
                    pe.wait_ge(xn_ready, at(b, c, 2, p + 1))
                    if not first:
                        if p == 0:
                            if attend:
                                pe.wait_ge(y_ready, at(b - 1, c - 1, 2, 2))
                            elif not (isinstance(b, int) and b == 0 and c == 1):
                                pe.wait_ge(res_ready, at(b, c - 2, 2, 2))
                        else:
                            if attend:
                                pe.wait_ge(out_ready, at(b - 1, c - 1, 2, 1))
                            else:
                                pe.wait_ge(xT_ready, at(b, c - 1, 2, 2))
                    for i in range(2):
                        for k in range(KT):
                            ins = nc.tensor.transpose(ps[:, XT[p], k * PAIR + i * P:k * PAIR + (i + 1) * P],
                                                      xn[:, 2 * p + i, k * P:(k + 1) * P], ident[:, :])
                    ins.then_inc(xT_done, 1)

            def three(dst, stat, mov):
                terms = [(0, 0), (1, 0), (0, 1)]
                for n, (s, m) in enumerate(terms):
                    for k in range(KT):
                        ins = nc.tensor.matmul(dst, stat(s, k), mov(m, k), start=(n == 0 and k == 0),
                                               stop=(n == len(terms) - 1 and k == KT - 1))
                return ins

            pe.wait_ge(consts, 6)
            transpose_x(0, 0, False, True)
            pe.wait_ge(kv_hi, 2)
            pe.wait_ge(kv_lo, 2)

            def query(b, c, i, banks):
                if i == 0:
                    pe.wait_ge(state_ready, b + 1)
                    pe.wait_ge(q_ready, at(b, c, 1, 1))
                for k in range(KT):
                    ins = nc.tensor.matmul(ps[:, banks[i], k * AW:(k + 1) * AW], q_sb[:, c, k, i * P:(i + 1) * P],
                                           state[:, k, :], start=True, stop=True)
                ins.then_inc(qkv_done, 1)

            def transpose_attn(b, c, p, banks):
                pe.wait_ge(attn_ready, at(b, c, TILES, 2 * p + 2))
                for i in range(2):
                    for k in range(KT):
                        ins = nc.tensor.transpose(ps[:, banks[p], k * PAIR + i * P:k * PAIR + (i + 1) * P],
                                                  attn[:, 2 * p + i, k * P:(k + 1) * P], ident[:, :])
                ins.then_inc(yT_done, 1)

            def project_y(b, c, p, banks):
                pe.wait_ge(yl_ready, at(b, c, 2, p + 1))
                for i in range(2):
                    t = slice((2 * p + i) * P, (2 * p + i + 1) * P)
                    ins = three(ps[:, banks[p], i * D:(i + 1) * D], lambda s, k: (yh, yl)[s][:, k, t],
                                lambda m, k: p_w[m][:, k, :])
                ins.then_inc(wp_done, 1)

            def step(b, c, attend, ahead):
                zero = isinstance(b, int) and b == 0
                past = not (zero and c == 0)
                x2 = [xh, xl]

                def project_kv(p):
                    pe.wait_ge(xl_ready, at(b, c, 2, p + 1))
                    if past:
                        pe.wait_ge(hid_ready, at(b, c - 1, J, J - p))
                    for i in range(2):
                        t = slice((2 * p + i) * P, (2 * p + i + 1) * P)
                        ins = three(ps[:, 2 * p + i, :], lambda s, k: x2[s][:, c, k, t], lambda m, k: kv_w[m][:, k, :])
                    ins.then_inc(kv_done, 1)

                def accumulate(p):
                    pe.wait_ge(k_ready, at(b, c, 2, p + 1))
                    pe.wait_ge(v_ready, at(b, c, 2, p + 1))
                    if c == 0 and p == 0 and not zero:
                        pe.wait_ge(state_ready, b)
                    for i in (2 * p, 2 * p + 1):
                        for k in range(KT):
                            ins = nc.tensor.matmul(ps[:, STATE, k * D:k * D + VW], k_sb[:, i, k * P:(k + 1) * P],
                                                   v_sb[:, i, k, :], start=(c == 0 and i == 0 and k == 0),
                                                   stop=(c == CB - 1 and i == TILES - 1), skip_group_check=True)
                    ins.then_inc(acc_done, 1)

                def project_q():
                    pe.wait_ge(v_ready, at(b, c, 2, 1))
                    if zero and c == 0:
                        pe.wait_ge(qp_hi, 1)
                        pe.wait_ge(qp_lo, 1)
                    for m in range(KT):
                        ins = three(ps[:, m, :], lambda s, k: q_w[s][:, k, m * P:(m + 1) * P],
                                    lambda s, k: x2[s][:, c, k, :])
                    ins.then_inc(q_done, 1)

                def gate_up(j):
                    if j == 0:
                        pe.wait_ge(v_ready, at(b, c, 2, 2))
                    elif j == 1:
                        pe.wait_ge(q_read, at(b, c, 1, 1))
                    else:
                        pe.wait_ge(hid_ready, at(b, c, J, j - 1))
                    for n, w in enumerate((g_w, u_w)):
                        dst = ps[:, gate_bank(j) + n, :]
                        cols = slice(j * P, (j + 1) * P)
                        for k in range(KT):
                            nc.tensor.matmul(dst, w[0][:, k, cols], xh[:, c, k, :], start=(k == 0), stop=False)
                    with pe.If(flag[0]):
                        pe.wait_ge(ffn_lo, NF)
                        for n, w in enumerate((g_w, u_w)):
                            for k in range(KT):
                                nc.tensor.matmul(ps[:, gate_bank(j) + n, :], w[1][:, k, j * P:(j + 1) * P],
                                                 xh[:, c, k, :], start=False, stop=False)
                    for n, w in enumerate((g_w, u_w)):
                        for k in range(KT):
                            ins = nc.tensor.matmul(ps[:, gate_bank(j) + n, :], w[0][:, k, j * P:(j + 1) * P],
                                                   xl[:, c, k, :], start=False, stop=(k == KT - 1))
                    ins.then_inc(gu_done, 1)

                def down(p, banks):
                    def both(h, w, j, start=False, stop=False):
                        for i in range(2):
                            t = slice((2 * p + i) * P, (2 * p + i + 1) * P)
                            ins = nc.tensor.matmul(ps[:, banks[p], i * D:(i + 1) * D], h[:, j, t], w[:, j, :],
                                                   start=start and i == 0, stop=stop, skip_group_check=True)
                        return ins

                    for j in range(J):
                        if p == 0:
                            pe.wait_ge(hh_ready, at(b, c, J, j + 1))
                        both(hh, d_w[0], j, start=(j == 0))
                    with pe.If(flag[0]):
                        for j in range(J):
                            both(hh, d_w[1], j)
                    for j in range(J):
                        if p == 0:
                            pe.wait_ge(hl_ready, at(b, c, J, j + 1))
                        ins = both(hl, d_w[0], j, stop=(j == J - 1))
                    ins.then_inc(down_done, 1)

                project_kv(0)
                if attend:
                    pe.wait_ge(xT_ready, at(b, c, 2, 2))
                    query(b - 1, c, 0, QKV)
                    pe.wait_ge(res_ready, at(b, c - 1, 2, 1))
                    query(b - 1, c, 1, QKV)
                project_kv(1)
                if attend:
                    pe.wait_ge(res_ready, at(b, c - 1, 2, 2))
                    query(b - 1, c, 2, QKV)
                    pe.wait_ge(attn_ready, at(b - 1, c, TILES, 1))
                    query(b - 1, c, 3, QKV)
                project_q()
                if attend:
                    transpose_attn(b - 1, c, 0, YT)
                    transpose_attn(b - 1, c, 1, YT)
                accumulate(0)
                accumulate(1)
                if not past:
                    pe.wait_ge(ffn_hi, 2)
                    pe.wait_ge(wide_seen, 1)
                    flag[0] = pe.value_load(wide_any[0:1, 0:1].bitcast(I32))
                gate_up(0)
                gate_up(1)
                if attend:
                    if isinstance(b, int) and b == 1 and c == 0:
                        pe.wait_ge(qp_hi, 2)
                        pe.wait_ge(qp_lo, 2)
                    project_y(b - 1, c, 0, WP)
                if ahead:
                    for j in range(2, J):
                        gate_up(j)
                    if attend:
                        project_y(b - 1, c, 1, WP)
                    nb, ncx = (b, 1) if c == 0 else (b + 1, 0)
                    transpose_x(nb, ncx, attend, False)
                    if attend:
                        pe.wait_ge(out_ready, at(b - 1, c, 2, 2))
                    elif past:
                        pe.wait_ge(res_ready, at(b, c - 1, 2, 1))
                    if not past:
                        pe.wait_ge(ffn_hi, 3)
                    down(0, DOWN)
                    pe.wait_ge(xT_ready, at(nb, ncx, 2, 1))
                    down(1, DOWN)
                else:
                    first, second = 0, 1
                    gate_up(2)
                    project_y(b - 1, c, 1, WP)
                    gate_up(3)
                    pe.wait_ge(y_ready, at(b - 1, c, 2, 2))
                    query(b, first, 0, LAST_QKV[0])
                    query(b, first, 1, LAST_QKV[0])
                    gate_up(4)
                    pe.wait_ge(out_ready, at(b - 1, c, 2, 1))
                    query(b, first, 2, LAST_QKV[0])
                    pe.wait_ge(out_ready, at(b - 1, c, 2, 2))
                    query(b, first, 3, LAST_QKV[0])
                    gate_up(5)
                    transpose_attn(b, first, 0, LAST_YT[0])
                    transpose_attn(b, first, 1, LAST_YT[0])
                    pe.wait_ge(hid_ready, at(b, c, J, 5))
                    query(b, second, 0, LAST_QKV[1])
                    query(b, second, 1, LAST_QKV[1])
                    down(0, LAST_DOWN)
                    pe.wait_ge(hid_ready, at(b, c, J, J))
                    query(b, second, 2, LAST_QKV[1])
                    query(b, second, 3, LAST_QKV[1])
                    project_y(b, first, 0, LAST_WP[0])
                    project_y(b, first, 1, LAST_WP[0])
                    transpose_attn(b, second, 0, LAST_YT[1])
                    transpose_attn(b, second, 1, LAST_YT[1])
                    down(1, LAST_DOWN)
                    project_y(b, second, 0, LAST_WP[1])
                    project_y(b, second, 1, LAST_WP[1])

            flag = [None]
            run(pe, step)


_T = ["L0_attn_Wq", "L0_attn_Wk", "L0_attn_Wv", "L0_attn_Wp", "L0_ffn_w_gate", "L0_ffn_w_up", "L0_ffn_w_down"]
_INS = ["L0_attn_x", "L0_attn_Wq", "L0_attn_Wk", "L0_attn_Wv", "L0_attn_Wp", "L0_attn_bp", "L0_attn_conv_w",
        "L0_attn_conv_b", "L0_ffn_w_gate", "L0_ffn_w_up", "L0_ffn_w_down"]


def kernel(**inputs):
    import numpy as _np
    import concourse.bacc as _bacc
    from concourse import mybir as _mybir
    from concourse.bass_utils import run_bass_kernel_spmd as _run

    nc = _bacc.Bacc("TRN2", target_bir_lowering=False, num_devices=1)
    arrays, args = {}, []
    for name in _INS:
        a = _np.asarray(inputs[name])
        a = _np.ascontiguousarray(a.T if name in _T else a)
        arrays[f"in_{name}_dram"] = a
        args.append(nc.dram_tensor(f"in_{name}_dram", a.shape, _mybir.dt.from_np(a.dtype), kind="ExternalInput").ap())
    x = arrays["in_L0_attn_x_dram"]
    out = nc.dram_tensor("out_0_dram", x.shape, _mybir.dt.from_np(x.dtype), kind="ExternalOutput").ap()
    build(nc, *args, out)
    r = _run(nc, [arrays], core_ids=[0])
    return r.results[0]["out_0_dram"]
```

```python
from contextlib import ExitStack

import concourse.bass as bass
from concourse import mybir

ALU = mybir.AluOpType
ACT = mybir.ActivationFunctionType
AX = mybir.AxisListType
F32 = mybir.dt.float32
F16 = mybir.dt.float16
I32 = mybir.dt.int32

P = 128
CHUNK = 512
TILES = CHUNK // P
PAIR = 2 * P
BANK = 512
HEADS = 16
EPS = 1e-5
FFN_SCALE = 1.0 / 127.0
EXPONENT = 0x7F800000
EXACT_INT = 2048.0

X_UP = 2.0 ** 10
W_UP = 2.0 ** 14
H_DOWN = 2.0 ** -20
TINY = 2.0 ** -96
WARM_UP = 40

D_SPLIT = 3
X_SPLIT = 4
Y_SPLIT = (2, 3)
Y_PROJECT = 4


def build(nc, x, wqT, wkT, wvT, wpT, bp, conv_w, conv_b, wgT, wuT, wdT, out):
    NB, S, D = x.shape
    HID = wgT.shape[1]
    KT = D // P
    J = HID // P
    HPB = HEADS // KT
    HD = D // HEADS
    CB = S // CHUNK
    AW = P + HPB
    VW = P + 1
    assert CB == 2 and KT == 2 and TILES == 4 and KT * D == BANK and KT * PAIR == BANK

    x_v = x.rearrange("b (c i p) d -> (b c) p i d", c=CB, p=P)
    out_v = out.rearrange("b (c i p) d -> (b c) p i d", c=CB, p=P)

    def at(b, c, per_step, k):
        return b * (CB * per_step) + (c * per_step + k)

    with ExitStack() as ctx:
        def sb(name, shape, dt=F32):
            return ctx.enter_context(nc.sbuf_tensor(name, shape, dt))

        def sem(name):
            return ctx.enter_context(nc.semaphore(name))

        names = ["q", "k", "v", "p"]
        w_raw = {n: sb(f"w{n}_raw", [P, KT, D]) for n in names}
        ffn_raw = {n: sb(f"w{n}_int", [P, HID * D // P], I32) for n in "gud"}
        kv_w = [sb(f"kv_w{h}", [P, KT, 2 * D], F16) for h in "hl"]
        q_w = [sb(f"q_w{h}", [P, KT, D], F16) for h in "hl"]
        p_w = [sb(f"p_w{h}", [P, KT, D], F16) for h in "hl"]
        g_w = [sb(f"g_w{h}", [P, KT, HID], F16) for h in "hl"]
        u_w = [sb(f"u_w{h}", [P, KT, HID], F16) for h in "hl"]
        d_w = [sb(f"d_w{h}", [P, J, D], F16) for h in "hl"]
        cw_raw = sb("cw_raw", [P, KT, 3])
        cb_raw = sb("cb_raw", [P, KT])
        cw = sb("cw", [P, KT, 3])
        cb = sb("cb", [P, KT])
        bp_sb = sb("bp_sb", [P, D])
        ident = sb("ident", [P, P])
        head_mask = sb("head_mask", [P, P])
        half = sb("half", [P, TILES])

        GROUPS = [["k", "v"], ["q"], ["g", "u"], ["d", "cw", "cb"], ["p"]]
        COL = {n: i for i, n in enumerate(sum(GROUPS, []))}
        maxima = sb("maxima", [P, len(COL)])
        over_all = sb("over_all", [P, len(COL)])
        power = sb("power", [P, len(COL)])
        scale_up = sb("scale_up", [P, len(COL)])
        wide = sb("wide", [P, 3])
        gate_up_wide = sb("gate_up_wide", [P, 1])
        scales = sb("scales", [P, 15])

        def col(of, name):
            return of[:, COL[name]:COL[name] + 1]

        def group(of, g):
            return of[:, COL[GROUPS[g][0]]:COL[GROUPS[g][-1]] + 1]

        (q_down, k_down, q_flip, k_flip, y_up, tap_up, attn_to_y, y_down, silu_in, h_mul, f_down,
         part_a, part_b, part_c, part_d) = (scales[:, i:i + 1] for i in range(15))

        x_in = sb("x_in", [P, CB, TILES, D])
        bn_raw = sb("bn_raw", [P, CB, TILES, 6])
        ln_tmp = sb("ln_tmp", [P, 5, TILES])
        neg_mean = sb("neg_mean", [P, CB, TILES])
        var_eps = sb("var_eps", [P, CB, TILES])
        rstd = sb("rstd", [P, CB, TILES])
        xn = sb("xn", [P, TILES, D])
        xb = sb("xb", [P, CB, TILES, D])
        xT = sb("xT", [P, CB, KT, CHUNK + 2])
        xn_h = sb("xn_h", [P, TILES, D], F16)
        xn_l = sb("xn_l", [P, TILES, D], F16)
        xh = sb("xh", [P, CB, TILES, KT, P], F16)
        xl = sb("xl", [P, CB, TILES, KT, P], F16)
        k_neg = sb("k_neg", [P, 2, 2, D])
        k_exp = sb("k_exp", [P, 2, 2, D])
        k_relu = sb("k_relu", [P, 2, 2, D])
        tap_part = [t[:, :, :, :].rearrange("p a b d -> p a (b d)") for t in (k_exp, k_relu)]
        k_sb = sb("k_sb", [P, TILES, D])
        v_sb = sb("v_sb", [P, TILES, KT, VW])
        q_neg = sb("q_neg", [P, KT, CHUNK])
        q_exp = sb("q_exp", [P, KT, CHUNK])
        q_relu = sb("q_relu", [P, KT, CHUNK])
        q_sb = sb("q_sb", [P, CB, KT, CHUNK])
        state = sb("state", [P, KT, AW])
        den = sb("den", [P, TILES, KT, HPB])
        rden = sb("rden", [P, TILES, KT, HPB])
        attn = sb("attn", [P, TILES, D])
        attn_h = sb("attn_h", [P, TILES, D], F16)
        attn_l = sb("attn_l", [P, TILES, D], F16)
        aT_h = sb("aT_h", [P, TILES, KT, P], F16)
        aT_l = sb("aT_l", [P, TILES, KT, P], F16)
        local = sb("local", [P, KT, S])
        y = sb("y", [P, KT, CHUNK])
        yh = sb("yh", [P, KT, CHUNK], F16)
        yl = sb("yl", [P, KT, CHUNK], F16)
        act_g = sb("act_g", [P, 2, CHUNK])
        hid = sb("hid", [P, 2, CHUNK])
        hh = sb("hh", [P, J, CHUNK], F16)
        hl = sb("hl", [P, J, CHUNK], F16)
        res = sb("res", [P, CB, TILES, D])
        out_sb = sb("out_sb", [P, CB, TILES, D])

        ps = ctx.enter_context(nc.psum_tensor("ps", [P, 8, BANK], F32))
        def gate_bank(j):
            return 2 * ((j + 1) % 2)
        STATE = 6
        QKV = [4, 5, 7, 4]
        WP = [4, 5]
        DOWN = [gate_bank(J - 2), QKV[2]]
        LAST_QKV = [[7, STATE, 4, 5], [2, 3, 0, 1]]
        LAST_YT = [[7, STATE], [2, 0]]
        LAST_WP = [[7, STATE], [3, 1]]
        LAST_DOWN = [4, 5]

        def halves(bank):
            return ps[:, bank, :].rearrange("p (k n) -> p k n", k=2)

        w_in = {n: sem(f"w{n}_loaded") for n in ["q", "k", "v", "p", "g", "u", "d"]}
        small_in = sem("small_loaded")
        consts = sem("consts_made")
        ones_made = sem("ones_made")
        maxed = [sem(f"group{g}_maxed") for g in range(len(GROUPS))]
        reduced = [sem(f"group{g}_reduced") for g in range(len(GROUPS))]
        scaled = [sem(f"group{g}_scaled") for g in range(len(GROUPS))]
        small_op = sem("scale_steps")
        k_hi, v_hi, kv_lo, q_hi, q_lo = sem("k_hi"), sem("v_hi"), sem("kv_lo"), sem("q_hi"), sem("q_lo")
        p_hi, p_lo, d_hi, d_lo = sem("p_hi"), sem("p_lo"), sem("d_hi"), sem("d_lo")
        gate_up_hi, gate_up_lo = sem("gate_up_hi"), sem("gate_up_lo")
        gate_up_seen, down_seen = sem("gate_up_wide_seen"), sem("down_wide_seen")
        taps_made = sem("taps_made")
        x_loaded = [sem(f"x_loaded{c}") for c in range(CB)]
        out_stored = [sem(f"out_stored{c}") for c in range(CB)]
        bn_seen, bn_merged, ln_ready = sem("bn_seen"), sem("bn_merged"), sem("ln_ready")
        bn_squared, bn_var = sem("bn_squared"), sem("bn_var")
        rstd_ready, xn_ready, xb_ready = sem("rstd_ready"), sem("xn_ready"), sem("xb_ready")
        xn_h_ready, xn_l_ready = sem("xn_h_ready"), sem("xn_l_ready")
        turns_due = sem("turns_due")
        xh_turned, xl_turned, xT_ready = sem("xh_turned"), sem("xl_turned"), sem("xT_ready")
        kv_done, k_parts, v_ready, k_ready = sem("kv_done"), sem("k_parts"), sem("v_ready"), sem("k_ready")
        acc_done, state_ready = sem("acc_done"), sem("state_ready")
        q_done, q_parts, q_ready = sem("q_done"), sem("q_parts"), sem("q_ready")
        k_flipped, q_flipped, q_read = sem("k_flipped"), sem("q_flipped"), sem("q_read")
        qkv_done, den_kept, den_inv, attn_ready = sem("qkv_done"), sem("den_kept"), sem("den_inv"), sem("attn_ready")
        attn_h_ready, attn_l_ready = sem("attn_h_ready"), sem("attn_l_ready")
        ah_turned, al_turned, y_begun = sem("ah_turned"), sem("al_turned"), sem("y_begun")
        yT_done, y_ready, yh_ready, yl_ready = sem("last_yT_done"), sem("y_ready"), sem("yh_ready"), sem("yl_ready")
        wp_done, out_ready = sem("wp_done"), sem("out_ready")
        gu_done, silu_ready, hid_ready = sem("gu_done"), sem("silu_ready"), sem("hid_ready")
        hh_ready, hl_ready, down_done, res_ready = sem("hh_ready"), sem("hl_ready"), sem("down_done"), sem("res_ready")
        tap_scaled = sem("tap_scaled")
        mid_tap, left_tap, conv_done = sem("mid_tap"), sem("left_tap"), sem("conv_done")

        block = ctx.enter_context(nc.Block())

        def run(eng, step):
            step(0, 0, False, True)
            step(0, 1, False, True)
            step(1, 0, True, True)
            step(1, 1, True, True)
            with eng.Fori(2, NB - 1) as b:
                step(b, 0, True, True)
                step(b, 1, True, True)
            step(NB - 1, 0, True, True)
            step(NB - 1, 1, True, False)

        @block.sync
        def _(sp):
            def load_weights(n, w, raw):
                sp.dma_start(raw, w.rearrange("(k p) n -> p k n", p=P)).then_inc(w_in[n], 16)

            def ffn_rows(n, w):
                return ffn_raw[n][:, :].rearrange("p (k n) -> p k n", n=w.shape[1])

            def turn(b, c, pairs, slot):
                for tokens, channels, ready, turned in pairs:
                    sp.wait_ge(ready, at(b, c, 2, 2))
                    sp.sem_inc(turns_due, 1)
                    sp.dma_start_transpose(slot(channels).rearrange("p i k t -> p (i k) t"),
                                           tokens[:, :, :].rearrange("p i d -> p (i d)")).then_inc(turned, 16)

            def turn_x(b, c):
                turn(b, c, [(xn_h, xh, xn_h_ready, xh_turned), (xn_l, xl, xn_l_ready, xl_turned)],
                     lambda channels: channels[:, c, :, :, :])

            def turn_attn(b, c):
                turn(b, c, [(attn_h, aT_h, attn_h_ready, ah_turned), (attn_l, aT_l, attn_l_ready, al_turned)],
                     lambda channels: channels[:, :, :, :])

            sp.dma_start(x_in[:, 0, :, :], x_v[0]).then_inc(x_loaded[0], 16)
            load_weights("q", wqT, w_raw["q"][:, :, :])
            load_weights("g", wgT, ffn_rows("g", wgT))
            load_weights("u", wuT, ffn_rows("u", wuT))
            sp.dma_start(bp_sb[:, :], bp.rearrange("(o n) -> o n", o=1).broadcast_to([P, D])).then_inc(small_in, 16)
            turn_x(0, 0)
            sp.dma_start(x_in[:, 1, :, :], x_v[1]).then_inc(x_loaded[1], 16)
            load_weights("d", wdT, ffn_rows("d", wdT))
            load_weights("p", wpT, w_raw["p"][:, :, :])
            sp.dma_start(cw_raw[:, :, :], conv_w.rearrange("(k p) t -> p k t", p=P)).then_inc(small_in, 16)
            sp.dma_start(cb_raw[:, :], conv_b.rearrange("(k p) -> p k", p=P),
                         allow_slow_non_contiguous=True).then_inc(small_in, 16)

            def store(b, c):
                sp.wait_ge(out_ready, at(b, c, 2, 2))
                sp.dma_start(out_v[b * CB + c], out_sb[:, c, :, :]).then_inc(out_stored[c], 16)

            def step(b, c, attend, ahead):
                if not (isinstance(b, int) and b == NB - 1):
                    if isinstance(b, int) and b == 0 and c == 0:
                        sp.wait_ge(xb_ready, 1)
                    sp.wait_ge(xn_ready, at(b, c, 2, 2))
                    sp.dma_start(x_in[:, c, :, :], x_v[CB * b + (c + CB)]).then_inc(x_loaded[c], 16)
                if attend:
                    turn_attn(b - 1, c)
                if ahead:
                    turn_x(*((b, 1) if c == 0 else (b + 1, 0)))
                if attend:
                    store(b - 1, c)

            run(sp, step)
            for c in range(CB):
                store(NB - 1, c)
            for c in range(CB):
                sp.wait_ge(out_stored[c], 16 * NB)

        @block.gpsimd
        def _(pool):
            def add_bias(b, c):
                nc.gpsimd.tensor_tensor(xb[:, c, :, :], x_in[:, c, :, :],
                                        bp_sb[:, :].unsqueeze(1).broadcast_to([P, TILES, D]),
                                        ALU.add).then_inc(xb_ready, 1)

            def normalise(c, i):
                return nc.gpsimd.tensor_scalar(xn[:, i, :], x_in[:, c, i, :], neg_mean[:, c, i:i + 1],
                                               rstd[:, c, i:i + 1], ALU.add, ALU.mult)

            def layernorm(b, c):
                pool.wait_ge(ln_ready, at(b, c, 1, 1))
                nc.gpsimd.tensor_tensor(rstd[:, c, :], var_eps[:, c, :], half[:, :], ALU.pow).then_inc(rstd_ready, 1)
                pool.wait_ge(rstd_ready, at(b, c, 1, 1))
                pool.wait_ge(xn_l_ready, at(b, c, 2, 0))
                add_bias(b, c)
                for i in range(TILES):
                    ins = normalise(c, i)
                    if i % 2 == 1:
                        ins.then_inc(xn_ready, 1)

            def put_xT(b, c):
                pool.wait_ge(xh_turned, at(b, c, 16, 16))
                pool.wait_ge(xl_turned, at(b, c, 16, 16))
                if not (isinstance(b, int) and b == 0):
                    pool.wait_ge(conv_done, at(b, c, KT, -KT))
                if c == 1:
                    nc.gpsimd.tensor_tensor(xT[:, 0, :, CHUNK + 1:CHUNK + 2], xh[:, 1, 0, :, 0:1],
                                            xl[:, 1, 0, :, 0:1], ALU.add)
                    nc.gpsimd.tensor_tensor(xT[:, 1, :, 0:1], xh[:, 0, TILES - 1, :, P - 1:P],
                                            xl[:, 0, TILES - 1, :, P - 1:P], ALU.add)
                nc.gpsimd.tensor_tensor(xT[:, c, :, 1:1 + CHUNK].rearrange("p k (i t) -> p i k t", i=TILES),
                                        xh[:, c, :, :, :], xl[:, c, :, :, :], ALU.add).then_inc(xT_ready, 1)

            def put_y(b, c, p):
                tiles, cols = slice(2 * p, 2 * p + 2), slice(p * PAIR, (p + 1) * PAIR)
                if p == 0:
                    pool.wait_ge(ah_turned, at(b, c, 16, 16))
                    pool.wait_ge(al_turned, at(b, c, 16, 16))
                    pool.wait_ge(conv_done, at(b, c, KT, KT))
                if not (isinstance(b, int) and b == 0 and c == 0):
                    pool.wait_ge(yl_ready, at(b, c, 2, p - 1))
                    pool.wait_ge(wp_done, at(b, c, 2, p - 1))
                nc.gpsimd.tensor_tensor(y[:, :, cols].rearrange("p k (i t) -> p i k t", i=2), aT_h[:, tiles, :, :],
                                        aT_l[:, tiles, :, :], ALU.add).then_inc(y_begun, 1)
                pool.wait_ge(y_begun, at(b, c, 2, p + 1))
                nc.gpsimd.tensor_tensor(y[:, :, cols], y[:, :, cols],
                                        local[:, :, c * CHUNK + p * PAIR:c * CHUNK + (p + 1) * PAIR],
                                        ALU.add).then_inc(y_ready, 1)

            def across(g):
                pool.wait_ge(maxed[g], len(GROUPS[g]))
                nc.gpsimd.partition_all_reduce(group(over_all, g), group(maxima, g), P,
                                               bass.bass_isa.ReduceOp.max).then_inc(reduced[g], 1)

            nc.gpsimd.memset(half[:, :], -0.5).then_inc(consts, 1)
            nc.gpsimd.memset(ident[:, :], 0.0).then_inc(consts, 1)
            nc.gpsimd.memset(head_mask[:, :], 1.0).then_inc(consts, 1)
            nc.gpsimd.memset(v_sb[:, :, :, P:VW], 1.0).then_inc(ones_made, 1)
            nc.gpsimd.memset(xT[:, 0, :, 0:1], 0.0).then_inc(ones_made, 1)
            nc.gpsimd.memset(xT[:, 1, :, CHUNK + 1:CHUNK + 2], 0.0).then_inc(ones_made, 1)
            pool.wait_ge(consts, 3)
            nc.gpsimd.affine_select(out=ident[:, :], in_=ident[:, :], compare_op=ALU.not_equal, fill=1.0,
                                    base=0, pattern=[[-1, P]], channel_multiplier=1).then_inc(consts, 1)
            hm = head_mask[:, :].rearrange("p (h e) -> p h e", h=HPB)
            nc.gpsimd.affine_select(out=hm, in_=hm, compare_op=ALU.is_ge, fill=0.0, base=0,
                                    pattern=[[-HD, HPB], [0, HD]], channel_multiplier=1).then_inc(consts, 1)
            pool.wait_ge(consts, 5)
            nc.gpsimd.affine_select(out=hm, in_=hm, compare_op=ALU.is_ge, fill=0.0, base=HD - 1,
                                    pattern=[[HD, HPB], [0, HD]], channel_multiplier=-1).then_inc(consts, 1)
            pool.wait_ge(ln_ready, 1)
            nc.gpsimd.tensor_tensor(rstd[:, 0, :], var_eps[:, 0, :], half[:, :], ALU.pow).then_inc(rstd_ready, 1)
            pool.wait_ge(rstd_ready, 1)
            normalise(0, 0)
            normalise(0, 1).then_inc(xn_ready, 1)
            across(0)
            normalise(0, 2)
            normalise(0, 3).then_inc(xn_ready, 1)
            across(1)
            across(2)
            put_xT(0, 0)
            pool.wait_ge(small_in, 48)
            add_bias(0, 0)

            def step(b, c, attend, ahead):
                if ahead:
                    nb, ncx = (b, 1) if c == 0 else (b + 1, 0)
                    layernorm(nb, ncx)
                if attend:
                    put_y(b - 1, c, 0)
                    put_y(b - 1, c, 1)
                if ahead:
                    if isinstance(b, int) and b == 0 and c == 0:
                        across(3)
                    put_xT(nb, ncx)
                if isinstance(b, int) and b == 0 and c == 0:
                    across(4)

            run(pool, step)
            for side, done, before in ((0, left_tap, mid_tap), (1, conv_done, left_tap)):
                for k in range(KT):
                    pool.wait_ge(tap_scaled, side * KT + k + 1)
                    pool.wait_ge(before, at(NB - 1, 1, KT, k + 1))
                    here = local[:, k, CHUNK:S]
                    nc.gpsimd.tensor_tensor(here, here, tap_part[side][:, k, :], ALU.add).then_inc(done, 1)

        @block.scalar
        def _(act):
            def x_high(b, c):
                for p in range(2):
                    act.wait_ge(xn_ready, at(b, c, 2, p + 1))
                    if p == 0 and not (isinstance(b, int) and b == 0 and c == 0):
                        act.wait_ge(xh_turned, at(b, c, 16, 0))
                    tiles = slice(2 * p, 2 * p + 2)
                    nc.scalar.activation(xn_h[:, tiles, :], xn[:, tiles, :], ACT.Copy).then_inc(xn_h_ready, 1)

            for n, w in (("k", wkT), ("v", wvT)):
                act.dma_start(w_raw[n][:, :, :], w.rearrange("(k p) n -> p k n", p=P)).then_inc(w_in[n], 16)
            nc.scalar.preload_act_table(ACT.Exp)

            def high(dst, src, name, done):
                g = [name in names for names in GROUPS].index(True)
                act.wait_ge(scaled[g], 1)
                nc.scalar.activation(dst, src, ACT.Copy, scale=col(scale_up, name)).then_inc(done, 1)

            x_high(0, 0)
            high(kv_w[0][:, :, 0:D], w_raw["k"][:, :, :], "k", k_hi)
            high(q_w[0][:, :, :], w_raw["q"][:, :, :], "q", q_hi)

            def middle_tap(b, c, k):
                if k == 0:
                    if not (isinstance(b, int) and b == 0):
                        act.wait_ge(y_ready, at(b - 1, c, 2, 2))
                    elif c == 0:
                        act.wait_ge(taps_made, 2)
                nc.scalar.activation(local[:, k, c * CHUNK:(c + 1) * CHUNK], xT[:, c, k, 1:1 + CHUNK],
                                     ACT.Identity, scale=cw[:, k, 1:2], bias=cb[:, k:k + 1]).then_inc(mid_tap, 1)

            def outer_tap(side, k):
                if side == 0 and k == 0:
                    act.wait_ge(k_ready, NB * CB * 2)
                nc.scalar.activation(tap_part[side][:, k, :], xT[:, 1, k, 2 * side:2 * side + CHUNK], ACT.Copy,
                                     scale=cw[:, k, 2 * side:2 * side + 1]).then_inc(tap_scaled, 1)

            def attn_high(b, c, p):
                tiles = slice(2 * p, 2 * p + 2)
                act.wait_ge(attn_ready, at(b, c, TILES, 2 * p + 2))
                if p == 0 and not (isinstance(b, int) and b == 0 and c == 0):
                    act.wait_ge(ah_turned, at(b, c, 16, 0))
                nc.scalar.activation(attn_h[:, tiles, :], attn[:, tiles, :], ACT.Copy,
                                     scale=attn_to_y).then_inc(attn_h_ready, 1)

            def y_high(b, c, p):
                cols = slice(p * PAIR, (p + 1) * PAIR)
                act.wait_ge(y_ready, at(b, c, 2, p + 1))
                nc.scalar.activation(yh[:, :, cols], y[:, :, cols], ACT.Copy).then_inc(yh_ready, 1)

            def step(b, c, attend, ahead):
                past = not (isinstance(b, int) and b == 0 and c == 0)

                def key_parts(p):
                    bank = 2 * p
                    act.wait_ge(kv_done, at(b, c, 2, p + 1))
                    if past:
                        act.wait_ge(k_ready, at(b, c - 1, 2, p + 1))
                    nc.scalar.activation(k_neg[:, p, :, :], ps[:, bank:bank + 2, 0:D], ACT.Relu,
                                         scale=k_flip).then_inc(k_flipped, 1)
                    nc.scalar.activation(k_relu[:, p, :, :], ps[:, bank:bank + 2, 0:D], ACT.Relu,
                                         scale=k_down)
                    if past:
                        act.wait_ge(acc_done, at(b, c - 1, 2, p + 1))
                    elif p == 0:
                        act.wait_ge(ones_made, 3)
                    for i in range(2):
                        ins = nc.scalar.activation(v_sb[:, 2 * p + i, :, 0:P],
                                                   ps[:, bank + i, D:2 * D].rearrange("p (k n) -> p k n", k=KT),
                                                   ACT.Copy)
                    ins.then_inc(v_ready, 1)
                    act.wait_ge(k_flipped, at(b, c, 2, p + 1))
                    nc.scalar.activation(k_exp[:, p, :, :], k_neg[:, p, :, :], ACT.Exp,
                                         scale=-1.0).then_inc(k_parts, 1)

                def query_parts():
                    act.wait_ge(q_done, at(b, c, 1, 1))
                    if past:
                        act.wait_ge(q_ready, at(b, c - 1, 1, 1))
                    nc.scalar.activation(q_neg[:, :, :], ps[:, 0:2, :], ACT.Relu, scale=q_flip).then_inc(q_flipped, 1)
                    act.wait_ge(q_flipped, at(b, c, 1, 1))
                    nc.scalar.activation(q_exp[:, :, :], q_neg[:, :, :], ACT.Exp, scale=-1.0).then_inc(q_parts, 1)

                def silu(j):
                    act.wait_ge(gu_done, at(b, c, J, j + 1))
                    if past or j >= 2:
                        act.wait_ge(hid_ready, at(b, c, J, j - 1))
                    nc.scalar.activation(act_g[:, j % 2, :], ps[:, gate_bank(j), :], ACT.Silu,
                                         scale=silu_in).then_inc(silu_ready, 1)

                def hidden_high(j):
                    act.wait_ge(hid_ready, at(b, c, J, j + 1))
                    if past and j == 0:
                        act.wait_ge(down_done, at(b, c - 1, 2, 2))
                    nc.scalar.activation(hh[:, j, :], hid[:, j % 2, :], ACT.Copy).then_inc(hh_ready, 1)

                if past:
                    act.wait_ge(xT_ready, at(b, c, 1, 1))
                    for k in range(KT):
                        middle_tap(*((b, 0) if c == 1 else (b - 1, 1)), k)
                key_parts(0)
                key_parts(1)
                if attend:
                    attn_high(b - 1, c, 0)
                    attn_high(b - 1, c, 1)
                query_parts()
                nc.scalar.preload_act_table(ACT.Silu)
                for j in range(J):
                    silu(j)
                    if j == J - 1 and past and not attend:
                        high(p_w[0][:, :, :], w_raw["p"][:, :, :], "p", p_hi)
                    if j == D_SPLIT and not past:
                        high(d_w[0][:, :, :], ffn_raw["d"][:, :].rearrange("p (k n) -> p k n", k=J), "d", d_hi)
                    if j >= 1:
                        hidden_high(j - 1)
                    if attend and j == Y_SPLIT[0]:
                        y_high(b - 1, c, 0)
                    if attend and j == Y_SPLIT[1]:
                        y_high(b - 1, c, 1)
                    if ahead and j == (X_SPLIT if attend else 1):
                        x_high(*((b, 1) if c == 0 else (b + 1, 0)))
                    if not ahead and j in (2, 4):
                        for k in range(KT):
                            outer_tap(j // 2 - 1, k)
                    if not ahead and j in (3, 4):
                        middle_tap(b, c, j - 3)
                hidden_high(J - 1)
                if ahead:
                    nc.scalar.preload_act_table(ACT.Exp)
                else:
                    for ac in range(CB):
                        y_high(b, ac, 0)
                        y_high(b, ac, 1)

            run(act, step)

        @block.vector
        def _(dve):
            def stats(b, c):
                dve.wait_ge(x_loaded[c], (b + 1) * 16)
                for i in range(TILES):
                    nc.vector.bn_stats(bn_raw[:, c, i, :], x_in[:, c, i, :]).then_inc(bn_seen, 1)
                even, odd = bn_raw[:, c, :, 0:3], bn_raw[:, c, :, 3:6]
                total, apart, spread, square, var = (ln_tmp[:, n, :] for n in range(5))
                dve.wait_ge(bn_seen, at(b, c, TILES, TILES))
                nc.vector.tensor_tensor(apart, even[:, :, 1], odd[:, :, 1], ALU.subtract)
                nc.vector.tensor_tensor(spread, even[:, :, 2], odd[:, :, 2], ALU.add)
                nc.vector.tensor_tensor(total, even[:, :, 1], odd[:, :, 1], ALU.add).then_inc(bn_merged, 1)
                dve.wait_ge(bn_merged, at(b, c, 1, 1))
                nc.vector.tensor_scalar(neg_mean[:, c, :], total, -0.5, None, ALU.mult)
                nc.vector.scalar_tensor_tensor(out=square, in0=apart, scalar=0.25, in1=apart, op0=ALU.mult,
                                               op1=ALU.mult).then_inc(bn_squared, 1)
                dve.wait_ge(bn_squared, at(b, c, 1, 1))
                nc.vector.scalar_tensor_tensor(out=var, in0=spread, scalar=1.0 / D, in1=square, op0=ALU.mult,
                                               op1=ALU.add).then_inc(bn_var, 1)
                dve.wait_ge(bn_var, at(b, c, 1, 1))
                nc.vector.tensor_scalar(var_eps[:, c, :], var, EPS, X_UP ** -2,
                                        ALU.add, ALU.mult).then_inc(ln_ready, 1)

            def x_low(b, c, p):
                dve.wait_ge(xn_h_ready, at(b, c, 2, p + 1))
                if p == 0 and not (isinstance(b, int) and b == 0 and c == 0):
                    dve.wait_ge(xl_turned, at(b, c, 16, 0))
                tiles = slice(2 * p, 2 * p + 2)
                nc.vector.tensor_tensor(xn_l[:, tiles, :], xn[:, tiles, :], xn_h[:, tiles, :],
                                        ALU.subtract).then_inc(xn_l_ready, 1)

            ops = [0]

            def scale_op(ins):
                ops[0] += 1
                ins.then_inc(small_op, 1)
                dve.wait_ge(small_op, ops[0])

            def powers(g):
                dve.wait_ge(reduced[g], 1)
                pow_, up = group(power, g), group(scale_up, g)
                scale_op(nc.vector.tensor_scalar(pow_, group(over_all, g), TINY, None, ALU.max))
                scale_op(nc.vector.tensor_scalar(pow_.bitcast(I32), pow_.bitcast(I32), EXPONENT, None,
                                                 ALU.bitwise_and))
                scale_op(nc.vector.reciprocal(up, pow_))
                scale_op(nc.vector.tensor_scalar(up, up, W_UP, None, ALU.mult))

            def maximum(n, src, dims):
                g = [n in names for names in GROUPS].index(True)
                nc.vector.tensor_reduce(col(maxima, n), src, dims, ALU.max,
                                        apply_absolute_value=True).then_inc(maxed[g], 1)

            def weight_maximum(n):
                dve.wait_ge(w_in[n], 16)
                if n in w_raw:
                    maximum(n, w_raw[n][:, :, :], AX.XY)
                else:
                    maximum(n, ffn_raw[n][:, :], AX.X)

            def low(dst, src, name, hi, halved, n, done):
                dve.wait_ge(halved, n)
                nc.vector.scalar_tensor_tensor(out=dst, in0=src, scalar=col(scale_up, name), in1=hi, op0=ALU.mult,
                                               op1=ALU.subtract).then_inc(done, 1)

            def ffn_blocks(n, k):
                return ffn_raw[n][:, :].rearrange("p (k n) -> p k n", k=k)

            def gate_up_high(n, w):
                nc.vector.tensor_scalar(w[0][:, :, :], ffn_blocks(n, KT), col(scale_up, n), None,
                                        ALU.mult).then_inc(gate_up_hi, 1)

            def feature_scales(n, flip, down):
                nc.vector.tensor_scalar(flip, col(power, n), -1.0 / (X_UP * W_UP), None, ALU.mult)
                return nc.vector.tensor_scalar(down, col(power, n), 1.0 / (X_UP * W_UP), None, ALU.mult)

            stats(0, 0)
            for n in ("k", "v", "q"):
                weight_maximum(n)
            x_low(0, 0, 0)
            powers(0)
            feature_scales("k", k_flip, k_down).then_inc(scaled[0], 1)
            x_low(0, 0, 1)
            nc.vector.tensor_scalar(kv_w[0][:, :, D:2 * D], w_raw["v"][:, :, :], col(scale_up, "v"), None,
                                    ALU.mult).then_inc(v_hi, 1)
            low(kv_w[1][:, :, D:2 * D], w_raw["v"][:, :, :], "v", kv_w[0][:, :, D:2 * D], v_hi, 1, kv_lo)
            low(kv_w[1][:, :, 0:D], w_raw["k"][:, :, :], "k", kv_w[0][:, :, 0:D], k_hi, 1, kv_lo)
            powers(1)
            feature_scales("q", q_flip, q_down).then_inc(scaled[1], 1)
            weight_maximum("g")
            weight_maximum("u")
            low(q_w[1][:, :, :], w_raw["q"][:, :, :], "q", q_w[0][:, :, :], q_hi, 1, q_lo)

            def gate_up_scales():
                powers(2)
                nc.vector.tensor_scalar(silu_in, col(power, "g"), FFN_SCALE / (X_UP * W_UP), None, ALU.mult)
                nc.vector.tensor_scalar(h_mul, col(scale_up, "g"), H_DOWN / W_UP, None, ALU.mult)
                scale_op(nc.vector.tensor_scalar(wide[:, 0:2], group(over_all, 2), EXACT_INT, None, ALU.is_gt))
                nc.vector.tensor_reduce(gate_up_wide[:, :], wide[:, 0:2], AX.X, ALU.max).then_inc(gate_up_seen, 1)

            def gate_up_low_halves():
                dve.wait_ge(gate_up_seen, 1)
                with dve.If(dve.value_load(gate_up_wide[0:1, 0:1].bitcast(I32))):
                    for i, (n, w) in enumerate((("g", g_w), ("u", u_w))):
                        low(w[1][:, :, :], ffn_blocks(n, KT), n, w[0][:, :, :], gate_up_hi, i + 1, gate_up_lo)

            def late_maxima():
                weight_maximum("d")
                dve.wait_ge(small_in, 48)
                maximum("cw", cw_raw[:, :, :], AX.XY)
                maximum("cb", cb_raw[:, :], AX.X)

            def down_scales():
                powers(3)
                scale_op(nc.vector.scalar_tensor_tensor(out=part_d, in0=col(power, "g"),
                                                        scalar=FFN_SCALE ** 2 / (H_DOWN * X_UP * W_UP * W_UP),
                                                        in1=col(power, "u"), op0=ALU.mult, op1=ALU.mult))
                nc.vector.tensor_scalar(wide[:, 2:3], col(over_all, "d"), EXACT_INT, None,
                                        ALU.is_gt).then_inc(down_seen, 1)
                nc.vector.tensor_tensor(f_down, part_d, col(power, "d"), ALU.mult).then_inc(scaled[3], 1)

            def down_low_half():
                dve.wait_ge(down_seen, 1)
                with dve.If(dve.value_load(wide[0:1, 2:3].bitcast(I32))):
                    low(d_w[1][:, :, :], ffn_blocks("d", J), "d", d_w[0][:, :, :], d_hi, 1, d_lo)

            def projection_scales():
                powers(4)
                nc.vector.scalar_tensor_tensor(out=y_down, in0=col(power, "p"), scalar=W_UP ** -2, in1=part_b,
                                               op0=ALU.mult, op1=ALU.mult).then_inc(scaled[4], 1)

            def attention_scales():
                scale_op(nc.vector.tensor_scalar(part_a, col(power, "v"), 512.0, None, ALU.mult))
                scale_op(nc.vector.scalar_tensor_tensor(out=part_b, in0=col(power, "cw"), scalar=128.0, in1=part_a,
                                                        op0=ALU.mult, op1=ALU.add))
                scale_op(nc.vector.scalar_tensor_tensor(out=part_a, in0=col(power, "cb"), scalar=2.0, in1=part_b,
                                                        op0=ALU.mult, op1=ALU.add))
                scale_op(nc.vector.tensor_scalar(part_b.bitcast(I32), part_a.bitcast(I32), EXPONENT, None,
                                                 ALU.bitwise_and))
                scale_op(nc.vector.reciprocal(part_c, part_b))
                scale_op(nc.vector.tensor_scalar(y_up, part_c, W_UP, None, ALU.mult))
                nc.vector.tensor_scalar(cb[:, :], cb_raw[:, :], y_up, None, ALU.mult).then_inc(taps_made, 1)
                nc.vector.scalar_tensor_tensor(out=attn_to_y, in0=col(power, "v"), scalar=1.0 / (X_UP * W_UP),
                                               in1=y_up, op0=ALU.mult, op1=ALU.mult)
                scale_op(nc.vector.tensor_scalar(tap_up, y_up, 1.0 / X_UP, None, ALU.mult))
                nc.vector.tensor_scalar(cw[:, :, :], cw_raw[:, :, :], tap_up, None, ALU.mult).then_inc(taps_made, 1)

            def normalise(b, c, p, banks):
                last = isinstance(b, int) and b == NB - 1 and c == 1
                if not last and not (isinstance(b, int) and b == 0 and c == 0):
                    dve.wait_ge(attn_l_ready, at(b, c, 2, p - 1))
                tiles = (2 * p, 2 * p + 1)
                src = {i: ps[:, banks[i], 0:KT * AW].rearrange("p (k n) -> p k n", k=KT) for i in tiles}
                for i in tiles:
                    dve.wait_ge(qkv_done, at(b, c, TILES, i + 1))
                    nc.vector.tensor_scalar(den[:, i, :, :], src[i][:, :, P:AW], 1e-6, None,
                                            ALU.max).then_inc(den_kept, 1)
                for i in tiles:
                    dve.wait_ge(den_kept, at(b, c, TILES, i + 1))
                    nc.vector.reciprocal(rden[:, i, :, :], den[:, i, :, :]).then_inc(den_inv, 1)
                for i in tiles:
                    dve.wait_ge(den_inv, at(b, c, TILES, i + 1))
                    nc.vector.tensor_tensor(attn[:, i, :].rearrange("p (k h e) -> p k h e", k=KT, h=HPB),
                                            src[i][:, :, 0:P].rearrange("p k (h e) -> p k h e", h=HPB),
                                            rden[:, i, :, :].unsqueeze(3).broadcast_to([P, KT, HPB, HD]),
                                            ALU.mult).then_inc(attn_ready, 1)

            def attn_low(b, c, p):
                tiles = slice(2 * p, 2 * p + 2)
                dve.wait_ge(attn_h_ready, at(b, c, 2, p + 1))
                if p == 0 and not (isinstance(b, int) and b == 0 and c == 0):
                    dve.wait_ge(al_turned, at(b, c, 16, 0))
                nc.vector.scalar_tensor_tensor(out=attn_l[:, tiles, :], in0=attn[:, tiles, :], scalar=attn_to_y,
                                               in1=attn_h[:, tiles, :], op0=ALU.mult,
                                               op1=ALU.subtract).then_inc(attn_l_ready, 1)

            def put_last_y(b, c, p, banks):
                cols = slice(p * PAIR, (p + 1) * PAIR)
                dve.wait_ge(yT_done, c * 2 + p + 1)
                if p == 0:
                    dve.wait_ge(conv_done, at(b, c, KT, KT))
                dve.wait_ge(yl_ready, at(b, c, 2, p - 1))
                dve.wait_ge(wp_done, at(b, c, 2, p - 1))
                nc.vector.scalar_tensor_tensor(out=y[:, :, cols], in0=halves(banks[p]), scalar=attn_to_y,
                                               in1=local[:, :, c * CHUNK + p * PAIR:c * CHUNK + (p + 1) * PAIR],
                                               op0=ALU.mult, op1=ALU.add).then_inc(y_ready, 1)

            def y_low(b, c, p):
                cols = slice(p * PAIR, (p + 1) * PAIR)
                dve.wait_ge(yh_ready, at(b, c, 2, p + 1))
                nc.vector.tensor_tensor(yl[:, :, cols], y[:, :, cols], yh[:, :, cols],
                                        ALU.subtract).then_inc(yl_ready, 1)

            def output(b, c, p, banks):
                dve.wait_ge(wp_done, at(b, c, 2, p + 1))
                dve.wait_ge(res_ready, at(b, c, 2, p + 1))
                if not (isinstance(b, int) and b == 0):
                    dve.wait_ge(out_stored[c], b * 16)
                nc.vector.scalar_tensor_tensor(out=out_sb[:, c, 2 * p:2 * p + 2, :], in0=halves(banks[p]),
                                               scalar=y_down, in1=res[:, c, 2 * p:2 * p + 2, :],
                                               op0=ALU.mult, op1=ALU.add).then_inc(out_ready, 1)

            def tap(b, c, k, side):
                done, before = (left_tap, mid_tap) if side == 0 else (conv_done, left_tap)
                dve.wait_ge(before, at(b, c, KT, k + 1))
                here = local[:, k, c * CHUNK:(c + 1) * CHUNK]
                nc.vector.scalar_tensor_tensor(out=here, in0=xT[:, c, k, side:side + CHUNK],
                                               scalar=cw[:, k, side:side + 1], in1=here,
                                               op0=ALU.mult, op1=ALU.add).then_inc(done, 1)

            def step(b, c, attend, ahead):
                past = not (isinstance(b, int) and b == 0 and c == 0)
                nb, ncx = (b, 1) if c == 0 else (b + 1, 0)
                if past:
                    pb, pc = (b, 0) if c == 1 else (b - 1, 1)

                def put_k(p):
                    dve.wait_ge(k_parts, at(b, c, 2, p + 1))
                    if past:
                        dve.wait_ge(acc_done, at(b, c - 1, 2, p + 1))
                    nc.vector.tensor_tensor(k_sb[:, 2 * p:2 * p + 2, :], k_exp[:, p, :, :], k_relu[:, p, :, :],
                                            ALU.add).then_inc(k_ready, 1)

                def relu_q():
                    dve.wait_ge(q_flipped, at(b, c, 1, 1))
                    if past:
                        dve.wait_ge(q_ready, at(b, c - 1, 1, 1))
                    nc.vector.tensor_scalar(q_relu[:, :, :], ps[:, 0:2, :], q_down, 0.0, ALU.mult,
                                            ALU.max).then_inc(q_read, 1)

                def put_q():
                    dve.wait_ge(q_parts, at(b, c, 1, 1))
                    dve.wait_ge(q_read, at(b, c, 1, 1))
                    nc.vector.tensor_tensor(q_sb[:, c, :, :], q_exp[:, :, :], q_relu[:, :, :],
                                            ALU.add).then_inc(q_ready, 1)

                def put_state():
                    dve.wait_ge(acc_done, at(b, c, 2, 2))
                    acc = halves(STATE)
                    for k in range(KT):
                        nc.vector.tensor_tensor(state[:, k, 0:P], acc[:, k, 0:P], head_mask[:, :], ALU.mult)
                        ins = nc.vector.tensor_scalar(state[:, k, P:AW], head_mask[:, 0:P:HD],
                                                      acc[:, k, P:P + 1], None, ALU.mult)
                    ins.then_inc(state_ready, 1)

                def hidden(j):
                    dve.wait_ge(silu_ready, at(b, c, J, j + 1))
                    if past or j >= 2:
                        dve.wait_ge(hl_ready, at(b, c, J, j - 1))
                    nc.vector.scalar_tensor_tensor(out=hid[:, j % 2, :], in0=act_g[:, j % 2, :], scalar=h_mul,
                                                   in1=ps[:, gate_bank(j) + 1, :], op0=ALU.mult,
                                                   op1=ALU.mult).then_inc(hid_ready, 1)

                def hidden_low(j):
                    dve.wait_ge(hh_ready, at(b, c, J, j + 1))
                    nc.vector.tensor_tensor(hl[:, j, :], hid[:, j % 2, :], hh[:, j, :],
                                            ALU.subtract).then_inc(hl_ready, 1)

                def put_res(p, banks):
                    dve.wait_ge(down_done, at(b, c, 2, p + 1))
                    dve.wait_ge(xb_ready, at(b, c, 1, 1))
                    if attend:
                        dve.wait_ge(out_ready, at(b - 1, c, 2, p + 1))
                    nc.vector.scalar_tensor_tensor(out=res[:, c, 2 * p:2 * p + 2, :], in0=halves(banks[p]),
                                                   scalar=f_down, in1=xb[:, c, 2 * p:2 * p + 2, :],
                                                   op0=ALU.mult, op1=ALU.add).then_inc(res_ready, 1)

                if past and not attend:
                    weight_maximum("p")
                if past:
                    tap(pb, pc, 0, 0)
                    tap(pb, pc, 1, 0)
                if past and ahead:
                    stats(nb, ncx)
                if attend:
                    normalise(b - 1, c, 0, QKV)
                put_k(0)
                if not past:
                    gate_up_high("g", g_w)
                    gate_up_high("u", u_w)
                if past:
                    tap(pb, pc, 0, 2)
                if attend:
                    normalise(b - 1, c, 1, QKV)
                if past:
                    tap(pb, pc, 1, 2)
                put_k(1)
                if not past:
                    stats(nb, ncx)
                if attend:
                    attn_low(b - 1, c, 0)
                    attn_low(b - 1, c, 1)
                relu_q()
                put_q()
                if not past:
                    late_maxima()
                    gate_up_low_halves()
                if ahead:
                    for j in range(J):
                        hidden(j)
                        if j >= 1:
                            hidden_low(j - 1)
                        if attend and j == Y_SPLIT[0]:
                            y_low(b - 1, c, 0)
                        if attend and j == Y_SPLIT[1]:
                            y_low(b - 1, c, 1)
                        if j == (X_SPLIT if attend else 1):
                            x_low(nb, ncx, 0)
                            x_low(nb, ncx, 1)
                        if j == 1 and not past:
                            down_scales()
                        if j == 3 and past and not attend:
                            projection_scales()
                    hidden_low(J - 1)
                    if c == CB - 1:
                        put_state()
                    if attend:
                        output(b - 1, c, 0, WP)
                        output(b - 1, c, 1, WP)
                    if past and not attend:
                        low(p_w[1][:, :, :], w_raw["p"][:, :, :], "p", p_w[0][:, :, :], p_hi, 1, p_lo)
                    if not past:
                        down_low_half()
                        attention_scales()
                    put_res(0, DOWN)
                    put_res(1, DOWN)
                else:
                    hidden(0)
                    hidden(1)
                    hidden_low(0)
                    put_state()
                    hidden(2)
                    hidden_low(1)
                    y_low(b - 1, c, 0)
                    hidden(3)
                    hidden_low(2)
                    y_low(b - 1, c, 1)
                    normalise(b, 0, 0, LAST_QKV[0])
                    hidden(4)
                    hidden_low(3)
                    output(b - 1, c, 0, WP)
                    output(b - 1, c, 1, WP)
                    hidden(5)
                    normalise(b, 0, 1, LAST_QKV[0])
                    hidden_low(4)
                    hidden_low(5)
                    put_last_y(b, 0, 0, LAST_YT[0])
                    put_last_y(b, 0, 1, LAST_YT[0])
                    y_low(b, 0, 0)
                    y_low(b, 0, 1)
                    normalise(b, 1, 0, LAST_QKV[1])
                    normalise(b, 1, 1, LAST_QKV[1])
                    put_res(0, LAST_DOWN)
                    put_last_y(b, 1, 0, LAST_YT[1])
                    put_last_y(b, 1, 1, LAST_YT[1])
                    output(b, 0, 0, LAST_WP[0])
                    output(b, 0, 1, LAST_WP[0])
                    y_low(b, 1, 0)
                    y_low(b, 1, 1)
                    put_res(1, LAST_DOWN)
                    output(b, 1, 0, LAST_WP[1])
                    output(b, 1, 1, LAST_WP[1])

            gate_up_scales()
            run(dve, step)

        @block.tensor
        def _(pe):
            def tiles_of(bank):
                return ps[:, bank, :].rearrange("p (i t) -> p i t", i=TILES)

            TERMS = [(0, 0), (1, 0), (0, 1)]

            def three(dst, stat, mov):
                for n, (s, m) in enumerate(TERMS):
                    for k in range(KT):
                        ins = nc.tensor.matmul(dst, stat(s, k), mov(m, k), start=(n == 0 and k == 0),
                                               stop=(n == len(TERMS) - 1 and k == KT - 1))
                return ins

            pe.wait_ge(consts, 6)
            for _ in range(WARM_UP):
                nc.tensor.matmul(ps[:, 3, 0:P], ident[:, :], ident[:, :], start=True, stop=True)

            def query(b, c, i, banks):
                if i == 0:
                    pe.wait_ge(state_ready, b + 1)
                    pe.wait_ge(q_ready, at(b, c, 1, 1))
                for k in range(KT):
                    ins = nc.tensor.matmul(ps[:, banks[i], k * AW:(k + 1) * AW], q_sb[:, c, k, i * P:(i + 1) * P],
                                           state[:, k, :], start=True, stop=True)
                ins.then_inc(qkv_done, 1)

            def transpose_attn(b, c, p, banks):
                pe.wait_ge(attn_ready, at(b, c, TILES, 2 * p + 2))
                for i in range(2):
                    for k in range(KT):
                        ins = nc.tensor.transpose(ps[:, banks[p], k * PAIR + i * P:k * PAIR + (i + 1) * P],
                                                  attn[:, 2 * p + i, k * P:(k + 1) * P], ident[:, :])
                ins.then_inc(yT_done, 1)

            def project_y(b, c, p, banks):
                pe.wait_ge(yl_ready, at(b, c, 2, p + 1))
                for i in range(2):
                    t = slice((2 * p + i) * P, (2 * p + i + 1) * P)
                    ins = three(ps[:, banks[p], i * D:(i + 1) * D], lambda s, k: (yh, yl)[s][:, k, t],
                                lambda m, k: p_w[m][:, k, :])
                ins.then_inc(wp_done, 1)

            def step(b, c, attend, ahead):
                zero = isinstance(b, int) and b == 0
                past = not (zero and c == 0)
                x2 = [xh, xl]

                def project_kv(p):
                    pe.wait_ge(xh_turned, at(b, c, 16, 16))
                    if not past:
                        pe.wait_ge(k_hi, 1)
                        pe.wait_ge(v_hi, 1)
                    if past and p == 0:
                        pe.wait_ge(hid_ready, at(b, c - 1, J, J))
                    elif past:
                        pe.wait_ge(res_ready, at(b, c - 1, 2, 1))
                    for n, (s, m) in enumerate(TERMS):
                        if n == 1:
                            pe.wait_ge(xl_turned, at(b, c, 16, 16))
                        elif n == 2 and not past:
                            pe.wait_ge(kv_lo, 2)
                        for i in range(2):
                            for k in range(KT):
                                ins = nc.tensor.matmul(ps[:, 2 * p + i, :], x2[s][:, c, 2 * p + i, k, :], kv_w[m][:, k, :],
                                                       start=(n == 0 and k == 0),
                                                       stop=(n == len(TERMS) - 1 and k == KT - 1))
                    ins.then_inc(kv_done, 1)

                def accumulate(p):
                    pe.wait_ge(k_ready, at(b, c, 2, p + 1))
                    pe.wait_ge(v_ready, at(b, c, 2, p + 1))
                    if c == 0 and p == 0 and not zero:
                        pe.wait_ge(state_ready, b)
                    for i in (2 * p, 2 * p + 1):
                        for k in range(KT):
                            ins = nc.tensor.matmul(ps[:, STATE, k * D:k * D + VW], k_sb[:, i, k * P:(k + 1) * P],
                                                   v_sb[:, i, k, :], start=(c == 0 and i == 0 and k == 0),
                                                   stop=(c == CB - 1 and i == TILES - 1), skip_group_check=True)
                    ins.then_inc(acc_done, 1)

                def project_q():
                    pe.wait_ge(v_ready, at(b, c, 2, 1))
                    if zero and c == 0:
                        pe.wait_ge(q_hi, 1)
                        pe.wait_ge(q_lo, 1)
                    for m in range(KT):
                        ins = three(tiles_of(m), lambda s, k: q_w[s][:, k, m * P:(m + 1) * P],
                                    lambda s, k: x2[s][:, c, :, k, :])
                    ins.then_inc(q_done, 1)

                def gate_up(j):
                    if j == 0:
                        pe.wait_ge(v_ready, at(b, c, 2, 2))
                    elif j == 1:
                        pe.wait_ge(q_read, at(b, c, 1, 1))
                    else:
                        pe.wait_ge(hid_ready, at(b, c, J, j - 1))
                    for n, w in enumerate((g_w, u_w)):
                        dst = tiles_of(gate_bank(j) + n)
                        cols = slice(j * P, (j + 1) * P)
                        for k in range(KT):
                            nc.tensor.matmul(dst, w[0][:, k, cols], xh[:, c, :, k, :], start=(k == 0), stop=False)
                    with pe.If(is_wide["gate_up"]):
                        pe.wait_ge(gate_up_lo, 2)
                        for n, w in enumerate((g_w, u_w)):
                            for k in range(KT):
                                nc.tensor.matmul(tiles_of(gate_bank(j) + n), w[1][:, k, j * P:(j + 1) * P],
                                                 xh[:, c, :, k, :], start=False, stop=False)
                    for n, w in enumerate((g_w, u_w)):
                        for k in range(KT):
                            ins = nc.tensor.matmul(tiles_of(gate_bank(j) + n), w[0][:, k, j * P:(j + 1) * P],
                                                   xl[:, c, :, k, :], start=False, stop=(k == KT - 1))
                    ins.then_inc(gu_done, 1)

                def down(p, banks):
                    def both(h, w, j, start=False, stop=False):
                        for i in range(2):
                            t = slice((2 * p + i) * P, (2 * p + i + 1) * P)
                            ins = nc.tensor.matmul(ps[:, banks[p], i * D:(i + 1) * D], h[:, j, t], w[:, j, :],
                                                   start=start and i == 0, stop=stop, skip_group_check=True)
                        return ins

                    for j in range(J):
                        if p == 0:
                            pe.wait_ge(hh_ready, at(b, c, J, j + 1))
                        both(hh, d_w[0], j, start=(j == 0))
                    with pe.If(is_wide["down"]):
                        pe.wait_ge(d_lo, 1)
                        for j in range(J):
                            both(hh, d_w[1], j)
                    for j in range(J):
                        if p == 0:
                            pe.wait_ge(hl_ready, at(b, c, J, j + 1))
                        ins = both(hl, d_w[0], j, stop=(j == J - 1))
                    ins.then_inc(down_done, 1)

                project_kv(0)
                if attend:
                    pe.wait_ge(res_ready, at(b, c - 1, 2, 1))
                    query(b - 1, c, 0, QKV)
                    query(b - 1, c, 1, QKV)
                project_kv(1)
                if attend:
                    pe.wait_ge(res_ready, at(b, c - 1, 2, 2))
                    query(b - 1, c, 2, QKV)
                    pe.wait_ge(attn_ready, at(b - 1, c, TILES, 1))
                    query(b - 1, c, 3, QKV)
                project_q()
                accumulate(0)
                accumulate(1)
                if not past:
                    pe.wait_ge(gate_up_hi, 2)
                    pe.wait_ge(gate_up_seen, 1)
                    is_wide["gate_up"] = pe.value_load(gate_up_wide[0:1, 0:1].bitcast(I32))
                gate_up(0)
                gate_up(1)
                if isinstance(b, int) and b == 1 and c == 0:
                    pe.wait_ge(p_hi, 1)
                    pe.wait_ge(p_lo, 1)
                if ahead:
                    for j in range(2, J):
                        gate_up(j)
                        if attend and j == Y_PROJECT:
                            project_y(b - 1, c, 0, WP)
                    if attend:
                        project_y(b - 1, c, 1, WP)
                    pe.wait_ge(hid_ready, at(b, c, J, J - 1))
                    if not past:
                        pe.wait_ge(d_hi, 1)
                        pe.wait_ge(down_seen, 1)
                        is_wide["down"] = pe.value_load(wide[0:1, 2:3].bitcast(I32))
                    down(0, DOWN)
                    if past and not attend:
                        pe.wait_ge(res_ready, at(b, c - 1, 2, 2))
                    down(1, DOWN)
                else:
                    first, second = 0, 1
                    gate_up(2)
                    gate_up(3)
                    pe.wait_ge(attn_ready, at(b - 1, c, TILES, 3))
                    query(b, first, 0, LAST_QKV[0])
                    query(b, first, 1, LAST_QKV[0])
                    project_y(b - 1, c, 0, WP)
                    gate_up(4)
                    project_y(b - 1, c, 1, WP)
                    gate_up(5)
                    pe.wait_ge(out_ready, at(b - 1, c, 2, 1))
                    query(b, first, 2, LAST_QKV[0])
                    pe.wait_ge(out_ready, at(b - 1, c, 2, 2))
                    query(b, first, 3, LAST_QKV[0])
                    transpose_attn(b, first, 0, LAST_YT[0])
                    transpose_attn(b, first, 1, LAST_YT[0])
                    pe.wait_ge(hid_ready, at(b, c, J, 5))
                    query(b, second, 0, LAST_QKV[1])
                    query(b, second, 1, LAST_QKV[1])
                    down(0, LAST_DOWN)
                    pe.wait_ge(hid_ready, at(b, c, J, J))
                    query(b, second, 2, LAST_QKV[1])
                    query(b, second, 3, LAST_QKV[1])
                    project_y(b, first, 0, LAST_WP[0])
                    project_y(b, first, 1, LAST_WP[0])
                    transpose_attn(b, second, 0, LAST_YT[1])
                    transpose_attn(b, second, 1, LAST_YT[1])
                    down(1, LAST_DOWN)
                    project_y(b, second, 0, LAST_WP[1])
                    project_y(b, second, 1, LAST_WP[1])

            is_wide = {}
            run(pe, step)


_T = ["L0_attn_Wq", "L0_attn_Wk", "L0_attn_Wv", "L0_attn_Wp", "L0_ffn_w_gate", "L0_ffn_w_up", "L0_ffn_w_down"]
_INS = ["L0_attn_x", "L0_attn_Wq", "L0_attn_Wk", "L0_attn_Wv", "L0_attn_Wp", "L0_attn_bp", "L0_attn_conv_w",
        "L0_attn_conv_b", "L0_ffn_w_gate", "L0_ffn_w_up", "L0_ffn_w_down"]


def kernel(**inputs):
    import numpy as _np
    import concourse.bacc as _bacc
    from concourse import mybir as _mybir
    from concourse.bass_utils import run_bass_kernel_spmd as _run

    nc = _bacc.Bacc("TRN2", target_bir_lowering=False, num_devices=1)
    arrays, args = {}, []
    for name in _INS:
        a = _np.asarray(inputs[name])
        a = _np.ascontiguousarray(a.T if name in _T else a)
        arrays[f"in_{name}_dram"] = a
        args.append(nc.dram_tensor(f"in_{name}_dram", a.shape, _mybir.dt.from_np(a.dtype), kind="ExternalInput").ap())
    x = arrays["in_L0_attn_x_dram"]
    out = nc.dram_tensor("out_0_dram", x.shape, _mybir.dt.from_np(x.dtype), kind="ExternalOutput").ap()
    build(nc, *args, out)
    r = _run(nc, [arrays], core_ids=[0])
    return r.results[0]["out_0_dram"]
```
